# Optimizing a Trainium2 kernel written in Bass

```python
import numpy as np
import jax
import jax.numpy as jnp

def _softmax(x, axis=-1):
    return jax.nn.softmax(x, axis=axis)

def _gelu(x):
    return jax.nn.gelu(x, approximate=True)

def _silu(x):
    return jax.nn.silu(x)

def _sigmoid(x):
    return jax.nn.sigmoid(x)

def _layernorm(x, axis=-1, eps=1e-05):
    m = jnp.mean(x, axis=axis, keepdims=True)
    v = jnp.var(x, axis=axis, keepdims=True)
    return (x - m) / jnp.sqrt(v + eps)

def _scatter_add(tgt, idx, src, axis=0):
    return tgt.at[idx].add(src)

def _segment_sum(src, seg, n):
    return jax.ops.segment_sum(src, seg, n)
kernel_name = 'mk_conv_preact_d4_conv_nchw8_r4_adc212'

def setup_inputs(seed: int=0):
    np.random.seed(seed)
    _w = jnp.asarray

    def _rec_inputs():
        import jax
        import jax.numpy as jnp
        _gk = jax.random.key(seed)
        x = -0.0003929 + 0.9999 * jax.random.normal(jax.random.fold_in(_gk, 1), (2, 8, 256, 256), jnp.float32)
        return x
    x = _rec_inputs()

    def _L0_conv_setup():
        import jax, jax.numpy as jnp
        import numpy as np
        B, E, N, D, H = (2, 8, 256, 256, 1024)
        key = jax.random.key(seed)
        k1, k2, k3 = jax.random.split(key, 3)
        x = jax.random.normal(k1, (B, E, N, D), dtype=jnp.float32)
        w1 = jax.random.normal(k2, (E, D, H), dtype=jnp.float32) * 0.02
        b1 = jnp.zeros((E, H), dtype=jnp.float32)
        w2 = jax.random.normal(k3, (E, H, D), dtype=jnp.float32) * 0.02
        b2 = jnp.zeros((E, D), dtype=jnp.float32)
        return {'x': x, 'w1': w1, 'b1': b1, 'w2': w2, 'b2': b2}
    _L0_conv_all = _L0_conv_setup()
    _L0_conv_in = {k: v for k, v in _L0_conv_all.items() if k in ('w1', 'b1', 'w2', 'b2')}
    del _L0_conv_all

    def _L1_conv_setup():
        import jax, jax.numpy as jnp
        import numpy as np
        from jax import lax
        TEMPERATURE = 1.0

        def binarize(w, temperature=TEMPERATURE):
            replace = jnp.clip(w, -1.0, 1.0)
            mean = jnp.mean(jnp.abs(w), axis=(-1, -2, -3), keepdims=True)
            binary = jnp.sign(jnp.clip(w / max(temperature, 0.0), -1.0, 1.0))
            return (lax.stop_gradient(binary - replace) + replace) * mean
        key = jax.random.key(seed)
        k1, k2, k3 = jax.random.split(key, 3)
        x = jax.random.normal(k1, (16, 8, 256, 256), dtype=jnp.float32)
        weight = jax.random.normal(k2, (8, 8, 3, 3), dtype=jnp.float32)
        bias = jax.random.normal(k3, (8,), dtype=jnp.float32)
        return {'x': x, 'weight': weight, 'bias': bias}
    _L1_conv_all = _L1_conv_setup()
    _L1_conv_in = {k: v for k, v in _L1_conv_all.items() if k in ('weight', 'bias')}
    del _L1_conv_all

    def _L2_conv_setup():
        import jax, jax.numpy as jnp
        import numpy as np
        B, E, N, D, H = (2, 8, 256, 256, 1024)
        key = jax.random.key(seed)
        k1, k2, k3 = jax.random.split(key, 3)
        x = jax.random.normal(k1, (B, E, N, D), dtype=jnp.float32)
        w1 = jax.random.normal(k2, (E, D, H), dtype=jnp.float32) * 0.02
        b1 = jnp.zeros((E, H), dtype=jnp.float32)
        w2 = jax.random.normal(k3, (E, H, D), dtype=jnp.float32) * 0.02
        b2 = jnp.zeros((E, D), dtype=jnp.float32)
        return {'x': x, 'w1': w1, 'b1': b1, 'w2': w2, 'b2': b2}
    _L2_conv_all = _L2_conv_setup()
    _L2_conv_in = {k: v for k, v in _L2_conv_all.items() if k in ('w1', 'b1', 'w2', 'b2')}
    del _L2_conv_all

    def _L3_conv_setup():
        import jax, jax.numpy as jnp
        import numpy as np
        B, E, N, D, F = (2, 8, 256, 256, 1024)
        key = jax.random.key(seed)
        k_x, k_w1, k_w2 = jax.random.split(key, 3)
        x = jax.random.normal(k_x, (B, E, N, D), dtype=jnp.float32)
        w1 = jax.random.normal(k_w1, (E, D, F), dtype=jnp.float32) * (1.0 / np.sqrt(D))
        b1 = jnp.zeros((E, F), dtype=jnp.float32)
        w2 = jax.random.normal(k_w2, (E, F, D), dtype=jnp.float32) * (1.0 / np.sqrt(F))
        b2 = jnp.zeros((E, D), dtype=jnp.float32)
        return {'x': x, 'w1': w1, 'b1': b1, 'w2': w2, 'b2': b2}
    _L3_conv_all = _L3_conv_setup()
    _L3_conv_in = {k: v for k, v in _L3_conv_all.items() if k in ('w1', 'b1', 'w2', 'b2')}
    del _L3_conv_all
    return {'x': x, 'L0_conv_w1': _L0_conv_in['w1'], 'L0_conv_b1': _L0_conv_in['b1'], 'L0_conv_w2': _L0_conv_in['w2'], 'L0_conv_b2': _L0_conv_in['b2'], 'L1_conv_weight': _L1_conv_in['weight'], 'L1_conv_bias': _L1_conv_in['bias'], 'L2_conv_w1': _L2_conv_in['w1'], 'L2_conv_b1': _L2_conv_in['b1'], 'L2_conv_w2': _L2_conv_in['w2'], 'L2_conv_b2': _L2_conv_in['b2'], 'L3_conv_w1': _L3_conv_in['w1'], 'L3_conv_b1': _L3_conv_in['b1'], 'L3_conv_w2': _L3_conv_in['w2'], 'L3_conv_b2': _L3_conv_in['b2']}

def reference(x, L0_conv_w1, L0_conv_b1, L0_conv_w2, L0_conv_b2, L1_conv_weight, L1_conv_bias, L2_conv_w1, L2_conv_b1, L2_conv_w2, L2_conv_b2, L3_conv_w1, L3_conv_b1, L3_conv_w2, L3_conv_b2):
    import jax
    import jax.numpy as jnp

    def _L0_conv_ref(x, w1, b1, w2, b2):
        import jax, jax.numpy as jnp
        import numpy as np
        B, E, N, D, H = (2, 8, 256, 256, 1024)
        h = jnp.einsum('bend,edh->benh', x, w1) + b1[None, :, None, :]
        h = jax.nn.gelu(h)
        out = jnp.einsum('benh,ehd->bend', h, w2) + b2[None, :, None, :]
        return out

    def _L1_conv_ref(x, weight, bias):
        import jax, jax.numpy as jnp
        import numpy as np
        from jax import lax
        TEMPERATURE = 1.0

        def binarize(w, temperature=TEMPERATURE):
            replace = jnp.clip(w, -1.0, 1.0)
            mean = jnp.mean(jnp.abs(w), axis=(-1, -2, -3), keepdims=True)
            binary = jnp.sign(jnp.clip(w / max(temperature, 0.0), -1.0, 1.0))
            return (lax.stop_gradient(binary - replace) + replace) * mean
        w = binarize(weight)
        xp = jnp.pad(x, ((0, 0), (0, 0), (1, 1), (1, 1)), mode='edge')
        out = lax.conv_general_dilated(xp, w, window_strides=(1, 1), padding='VALID', lhs_dilation=(1, 1), rhs_dilation=(1, 1), dimension_numbers=('NCHW', 'OIHW', 'NCHW'), feature_group_count=1)
        return out + bias[None, :, None, None]

    def _L2_conv_ref(x, w1, b1, w2, b2):
        import jax, jax.numpy as jnp
        import numpy as np
        B, E, N, D, H = (2, 8, 256, 256, 1024)
        h = jnp.einsum('bend,edh->benh', x, w1) + b1[None, :, None, :]
        h = jax.nn.gelu(h)
        out = jnp.einsum('benh,ehd->bend', h, w2) + b2[None, :, None, :]
        return out

    def _L3_conv_ref(x, w1, b1, w2, b2):
        import jax, jax.numpy as jnp
        import numpy as np
        B, E, N, D, F = (2, 8, 256, 256, 1024)
        h = jnp.einsum('bend,edf->benf', x, w1) + b1[None, :, None, :]
        h = jax.nn.gelu(h, approximate=False)
        out = jnp.einsum('benf,efd->bend', h, w2) + b2[None, :, None, :]
        return out

    def _gn(v, G=4, eps=1e-05):
        B_, C_, H_, W_ = v.shape
        g = v.reshape(B_, G, C_ // G, H_, W_)
        m = jnp.mean(g, axis=(2, 3, 4), keepdims=True)
        s = jnp.var(g, axis=(2, 3, 4), keepdims=True)
        return ((g - m) / jnp.sqrt(s + eps)).reshape(v.shape)

    def _ln_c(v, eps=1e-06):
        m = jnp.mean(v, axis=1, keepdims=True)
        s = jnp.var(v, axis=1, keepdims=True)
        return (v - m) / jnp.sqrt(s + eps)

    def _ln_t(v, eps=1e-05):
        m = jnp.mean(v, axis=-1, keepdims=True)
        s = jnp.var(v, axis=-1, keepdims=True)
        return (v - m) / jnp.sqrt(s + eps)

    def _to_tokens(v):
        B_, C_, H_, W_ = v.shape
        return v.reshape(B_, C_, H_ * W_).transpose(0, 2, 1)

    def _from_tokens(t, like):
        B_, C_, H_, W_ = like.shape
        return t.transpose(0, 2, 1).reshape(B_, C_, H_, W_)
    x = x + _L0_conv_ref(_gn(x), L0_conv_w1, L0_conv_b1, L0_conv_w2, L0_conv_b2)
    x = x + _L1_conv_ref(_gn(x), L1_conv_weight, L1_conv_bias)
    x = x + _L2_conv_ref(_gn(x), L2_conv_w1, L2_conv_b1, L2_conv_w2, L2_conv_b2)
    x = x + _L3_conv_ref(_gn(x), L3_conv_w1, L3_conv_b1, L3_conv_w2, L3_conv_b2)
    return x

_drawn_inputs = setup_inputs


def setup_inputs(seed=0):
    import zlib

    import numpy as np

    out = dict(_drawn_inputs(seed))
    spreads = {'L0_conv_b1': (0.0, 0.1),
     'L0_conv_b2': (0.0, 0.1),
     'L2_conv_b1': (0.0, 0.8),
     'L2_conv_b2': (0.0, 0.594),
     'L3_conv_b1': (0.0, 0.8),
     'L3_conv_b2': (0.0, 0.579)}
    factors = {'L2_conv_w1': 3.768, 'L2_conv_w2': 3.505}
    for name, (base, spread) in spreads.items():
        noise = np.random.default_rng([zlib.crc32(name.encode()), seed]).standard_normal(out[name].shape)
        drawn = base * np.exp(spread * noise) if base else spread * noise
        out[name] = jnp.asarray(drawn.astype(out[name].dtype))
    for name, factor in factors.items():
        out[name] = (out[name] * factor).astype(out[name].dtype)
    return out
```

```python
from contextlib import ExitStack

import concourse.bass as bass
import concourse.mybir as mybir

F32 = mybir.dt.float32
F32R = mybir.dt.float32r
ALU = mybir.AluOpType
ACT = mybir.ActivationFunctionType
AX = mybir.AxisListType

B, C, N, D, H = 2, 8, 256, 256, 1024
PART = 128
DC = D // PART
NC = N // PART
TOK = B * N
HT = H // PART
NPAIR = C // 2
LAYERS = 3
BCOLS = C * HT + C * DC
GN_EPS = 1e-5
RING = 4

KS = 3
ROWS = PART // C
OUTR = ROWS - (KS - 1)
NBLK = -(-D // OUTR)
LASTROW = D + 2 - ROWS
NP = N + 2
DP = D + 2
STORES = [(0, 5), (5, 10), (10, 15), (15, 18)]
JOBS = 4 * NPAIR


def build(nc, x, w1, b1, w2, b2, cw, cb, out):
    x1_dram = nc.dram_tensor("x1_scratch", (C, DP, TOK), F32, kind="Internal").ap()
    x2_dram = nc.dram_tensor("x2_scratch", (C, D, TOK), F32, kind="Internal").ap()

    with ExitStack() as ctx:
        def sb(name, shape, dt=F32, where=ctx):
            return where.enter_context(nc.sbuf_tensor(name, shape, dt))

        def bank(name):
            return ctx.enter_context(nc.psum_tensor(name, [PART, 512], F32))

        def sem(name):
            return ctx.enter_context(nc.semaphore(name))

        XT = sb("XT", [PART, C, DC, B, N])
        W1raw = sb("W1raw", [PART, DC, H])
        W2raw = sb("W2raw", [PART, HT, D])
        W1h = sb("W1h", [PART, 2, DC, H], F32R)
        W1l = sb("W1l", [PART, 2, DC, H], F32R)
        W2h = sb("W2h", [PART, 2, HT, D], F32R)
        W2l = sb("W2l", [PART, 2, HT, D], F32R)
        XN = sb("XN", [PART, B, DC, N])
        Xh = sb("Xh", [PART, 2, DC, B, N], F32R)
        Xl = sb("Xl", [PART, 2, DC, B, N], F32R)
        ident = sb("ident", [PART, PART])
        ones_mean = sb("ones_mean", [PART, PART])
        half = sb("half", [PART, B])
        bias_rows = sb("bias_rows", [BCOLS, LAYERS, PART])
        BT = sb("BT", [PART, LAYERS * BCOLS])
        BN = sb("BN", [PART, B, 2, 6])
        MV = sb("MV", [PART, B, 2])
        MEAN = sb("MEAN", [PART, B])
        DM = sb("DM", [PART, B])
        Q = sb("Q", [PART, B])
        VE = sb("VE", [PART, B])
        RS = sb("RS", [PART, B])
        ST = sb("ST", [PART, NPAIR + 1, 2 * B])
        CST = sb("CST", [PART, 2 * B])
        conv_rep = sb("conv_rep", [PART, C, KS * KS])
        conv_out = sb("conv_out", [PART, C * KS * KS])
        conv_bias = sb("conv_bias", [PART, 1])
        conv_mean = sb("conv_mean", [PART, 1])
        conv_abs = sb("conv_abs", [PART, C * KS * KS])
        conv_sum = sb("conv_sum", [PART, 1])
        conv_neg = sb("conv_neg", [PART, C, KS * KS])
        conv_sign = sb("conv_sign", [PART, C, KS * KS])
        diag = sb("diag", [PART, KS, C, ROWS])
        mask = sb("mask", [PART, KS, ROWS])
        band_tap = sb("band_tap", [PART, KS, C, ROWS])
        band_sum = sb("band_sum", [PART, C, ROWS])
        BAND = sb("BAND", [PART, KS, C, ROWS], F32R)

        with ExitStack() as use:
            NAT = sb("NAT", [PART, NPAIR, B, 2, NC, D], F32, use)
        with ExitStack() as use:
            XFIN = sb("XFIN", [PART, 2, DC, B, N], F32, use)
            OUTT = sb("OUTT", [PART, B, NC, D], F32, use)
        XC = sb("XC", [PART, NBLK, B, NP])

        with ExitStack() as use:
            HR = sb("HR", [PART, 2, TOK], F32, use)
            Hh = sb("Hh", [PART, RING, TOK], F32R, use)
            Hl = sb("Hl", [PART, RING, TOK], F32R, use)
        CN = sb("CN", [PART, 2, B, NP])
        Ch = sb("Ch", [PART, RING, B, NP], F32R)
        Cl = sb("Cl", [PART, RING, B, NP], F32R)

        G1 = [bank(f"G1_{i}") for i in range(2)]
        ACC = [[bank(f"ACC_{i}_{m}") for m in range(DC)] for i in range(2)]
        STAT = bank("STAT")
        TR = bank("TR")
        ROT = [ACC[0][0], ACC[0][1], ACC[1][0], ACC[1][1]]

        x_in = [sem(f"x_in{g}") for g in range(NPAIR)]
        w1_in, w2_in, bias_in, conv_in = sem("w1_in"), sem("w2_in"), sem("bias_in"), sem("conv_in")
        consts, diag_zero = sem("consts"), sem("diag_zero")
        in_tr, in_evac_act, in_evac_dve = sem("in_tr"), sem("in_evac_act"), sem("in_evac_dve")
        bias_tr, bias_t = sem("bias_tr"), sem("bias_t")
        bn_done, mv_done, mean_mm, dm_done = sem("bn_done"), sem("mv_done"), sem("mean_mm"), sem("dm_done")
        q_done, var_mm, ve_done, rs_done, st_done = (sem("q_done"), sem("var_mm"), sem("ve_done"), sem("rs_done"),
                                                     sem("st_done"))
        whi, wlo = sem("whi"), sem("wlo")
        xn_done, xhi, xlo = sem("xn_done"), sem("xhi"), sem("xlo")
        g1_done, gelu_done, hhi, hlo, g2_done = (sem("g1_done"), sem("gelu_done"), sem("hhi"), sem("hlo"),
                                                 sem("g2_done"))
        evicted = sem("evicted")
        prep = sem("prep")
        x1_out, xc_in = sem("x1_out"), sem("xc_in")
        cst_done, pads = sem("cst_done"), sem("pads")
        cn_done, chi, clo, conv_mm, cscaled, cadded = (sem("cn_done"), sem("chi"), sem("clo"), sem("conv_mm"),
                                                       sem("cscaled"), sem("cadded"))
        x2_out, x2_first, x2_rest = sem("x2_out"), sem("x2_first"), sem("x2_rest")
        out_tr, out_evac = sem("out_tr"), sem("out_evac")
        out_st = [sem(f"out_st{b}") for b in range(B)]

        block = ctx.enter_context(nc.Block())

        def wait(eng, s, value):
            if not isinstance(value, int) or value > 0:
                eng.wait_ge(s, value)

        def job_of(P, ee, conv_layer):
            if isinstance(P, int):
                table = {(0, 0): 1, (1, 0): 2, (1, 1): 3, (2, 0): 4, (2, 1): 5, (3, 1): 6}
                if P < NPAIR:
                    return table.get((P, ee))
                return P + 5 if ee == 0 and P + 1 < LAYERS * NPAIR else None
            if conv_layer:
                return 2 * P + ee
            return P + 5 if ee == 0 else None

        @block.sync
        def _(sp):
            def load_x(g):
                for b in range(B):
                    sp.dma_start(NAT[:, g, b], x[b, 2 * g:2 * g + 2].rearrange("e (c p) d -> p e c d", p=PART)
                                 ).then_inc(x_in[g], 16)

            def load_w1(f, e, E):
                wait(sp, wlo, 8 * E - 4)
                sp.dma_start(W1raw[:], w1[f][e].rearrange("(c p) h -> p c h", p=PART)).then_inc(w1_in, 16)

            def load_w2(f, e, E):
                wait(sp, wlo, 8 * E)
                sp.dma_start(W2raw[:], w2[f][e].rearrange("(t p) d -> p t d", p=PART)).then_inc(w2_in, 16)

            load_x(0)
            load_w1(0, 0, 0)
            load_w2(0, 0, 0)
            for f in range(LAYERS):
                sp.dma_start(bias_rows[0:C * HT, f, :], b1[f].rearrange("e (t p) -> (e t) p", p=PART)
                             ).then_inc(bias_in, 16)
                sp.dma_start(bias_rows[C * HT:BCOLS, f, :], b2[f].rearrange("e (c p) -> (e c) p", p=PART)
                             ).then_inc(bias_in, 16)
            for g in range(1, NPAIR):
                load_x(g)
            for ci in range(C):
                own = slice(ci * ROWS, (ci + 1) * ROWS)
                sp.dma_start(conv_rep[own], cw[:, ci].rearrange("o a b -> o (a b)").unsqueeze(0)
                             .broadcast_to([ROWS, C, KS * KS])).then_inc(conv_in, 16)
                sp.dma_start(conv_out[own], cw[ci:ci + 1].rearrange("o i a b -> o (i a b)")
                             .broadcast_to([ROWS, C * KS * KS])).then_inc(conv_in, 16)
                sp.dma_start(conv_bias[own], cb[ci:ci + 1].unsqueeze(0).broadcast_to([ROWS, 1])
                             ).then_inc(conv_in, 16)

            def store_x1(e):
                sp.wait_ge(evicted, 2 * e + 2)
                sp.dma_start(x1_dram[e, 1:D + 1].rearrange("(c p) t -> p c t", p=PART),
                             XT[:, e].rearrange("p c b n -> p c (b n)")).then_inc(x1_out, 16)
                sp.dma_start(x1_dram[e, 0:1], XT[0:1, e, 0].rearrange("p b n -> p (b n)")).then_inc(x1_out, 16)
                sp.dma_start(x1_dram[e, D + 1:DP], XT[PART - 1:PART, e, DC - 1].rearrange("p b n -> p (b n)")
                             ).then_inc(x1_out, 16)

            def load_xc(e):
                if e == 0:
                    sp.wait_ge(in_tr, B * C)
                sp.wait_ge(x1_out, 48 * (e + 1))
                own = slice(e * ROWS, (e + 1) * ROWS)
                for b in range(B):
                    src = x1_dram[e, 0:OUTR * (NBLK - 1), b * N:(b + 1) * N].rearrange("(k j) n -> j k n", j=OUTR)
                    sp.dma_start(XC[own.start:own.start + OUTR, 0:NBLK - 1, b, 1:N + 1], src).then_inc(xc_in, 16)
                    tail = x1_dram[e, OUTR:OUTR * NBLK - OUTR + 0, b * N:(b + 1) * N]
                    src = tail.rearrange("(k j) n -> j k n", j=OUTR)[0:KS - 1]
                    sp.dma_start(XC[own.start + OUTR:own.stop, 0:NBLK - 2, b, 1:N + 1], src).then_inc(xc_in, 16)
                    sp.dma_start(XC[own.start + OUTR:own.stop, NBLK - 2, b, 1:N + 1],
                                 x1_dram[e, OUTR * (NBLK - 1):OUTR * (NBLK - 1) + KS - 1, b * N:(b + 1) * N]
                                 ).then_inc(xc_in, 16)
                    sp.dma_start(XC[own, NBLK - 1, b, 1:N + 1], x1_dram[e, LASTROW:DP, b * N:(b + 1) * N]
                                 ).then_inc(xc_in, 16)

            for E in range(1, C + 2):
                f, e = divmod(E, C)
                if E >= 3:
                    store_x1(E - 3)
                load_w1(f, e, E)
                if E >= 3:
                    load_xc(E - 3)
                load_w2(f, e, E)
            store_x1(C - 1)
            load_xc(C - 1)

            n_stores = 0
            for k0, k1 in STORES + [(NBLK - 1, NBLK)]:
                sp.wait_ge(cadded, k1)
                for o in range(C):
                    if k0 < NBLK - 1:
                        dst = x2_dram[o, OUTR * k0:OUTR * k1].rearrange("(k j) (b n) -> j k b n", j=OUTR, b=B)
                        own = slice(o * ROWS + 1, o * ROWS + 1 + OUTR)
                        for b in range(B):
                            sp.dma_start(dst[:, :, b], XC[own, k0:k1, b, 1:N + 1]).then_inc(x2_out, 16)
                            n_stores += 1
                    else:
                        r0 = OUTR * k0
                        own = slice(o * ROWS + 1 + r0 - LASTROW, o * ROWS + 1 + OUTR)
                        sp.dma_start(x2_dram[o, r0:D].rearrange("r (b n) -> r b n", b=B), XC[own, k0, :, 1:N + 1]
                                     ).then_inc(x2_out, 16)
                        n_stores += 1
            sp.wait_ge(x2_out, 16 * n_stores)
            for e in range(C):
                sp.dma_start(XT[:, e].rearrange("p c b n -> p c (b n)"),
                             x2_dram[e].rearrange("(c p) t -> p c t", p=PART)
                             ).then_inc(x2_first if e < 2 else x2_rest, 16)

            with sp.Fori(2, C) as e:
                load_w1(1, e, C + e)
                load_w2(1, e, C + e)

            def store_out(e, b, n):
                wait(sp, out_evac, 2 * n - 1 + b)
                sp.dma_start(out[b, e].rearrange("(c p) d -> p c d", p=PART), OUTT[:, b]).then_inc(out_st[b], 16)

            with sp.Fori(0, 3) as e:
                load_w1(2, e, 2 * C + e)
                load_w2(2, e, 2 * C + e)
            with sp.Fori(3, C) as e:
                load_w1(2, e, 2 * C + e)
                store_out(e - 3, 0, e - 2)
                load_w2(2, e, 2 * C + e)
                store_out(e - 3, 1, e - 2)
            for e in range(C - 3, C):
                for b in range(B):
                    store_out(e, b, e + 1)
            for b in range(B):
                sp.wait_ge(out_st[b], 16 * C)

        @block.gpsimd
        def _(pool):
            nc.gpsimd.memset(ident[:], 0.0).then_inc(diag_zero, 1)
            nc.gpsimd.memset(ones_mean[:], 1.0 / PART).then_inc(consts, 1)
            nc.gpsimd.memset(half[:], -0.5).then_inc(consts, 1)
            nc.gpsimd.memset(diag[:], 0.0).then_inc(diag_zero, 1)
            pool.wait_ge(diag_zero, 1)
            nc.gpsimd.affine_select(out=ident[:], in_=ident[:], compare_op=ALU.not_equal, fill=1.0, base=0,
                                    pattern=[[-1, PART]], channel_multiplier=1).then_inc(consts, 1)
            pool.wait_ge(diag_zero, 2)
            for kw in range(KS):
                nc.gpsimd.affine_select(out=diag[:, kw], in_=diag[:, kw], compare_op=ALU.not_equal, fill=1.0,
                                        base=1 - kw, pattern=[[-ROWS, C], [-1, ROWS]], channel_multiplier=1
                                        ).then_inc(consts, 1)

            def rstd(J):
                wait(pool, ve_done, J + 1)
                nc.gpsimd.tensor_tensor(RS[:], VE[:], half[:], ALU.pow).then_inc(rs_done, 1)

            with pool.Fori(0, 2 * NPAIR) as J:
                rstd(J)

            def normalise_block(k):
                wait(pool, clo, k - 1)
                for b in range(B):
                    ins = nc.gpsimd.tensor_scalar(CN[:, k % 2, b], XC[:, k, b], CST[:, b:b + 1],
                                                  CST[:, B + b:B + b + 1], ALU.mult, ALU.add)
                ins.then_inc(cn_done, 1)

            pool.wait_ge(cst_done, NPAIR)
            pool.wait_ge(pads, 2)
            for k in range(NBLK):
                normalise_block(k)

            with pool.Fori(2 * NPAIR, JOBS) as J:
                rstd(J)

        @block.scalar
        def _(act):
            for i in range(0, B * C, 2):
                e, b = divmod(i, B)
                act.wait_ge(in_tr, i + 1)
                nc.scalar.activation(XT[:, e, :, b], ROT[i % 4][:].rearrange("p (c n) -> p c n", c=DC), ACT.Copy
                                     ).then_inc(in_evac_act, 1)

            def w_hi(E, par, k):
                if k < 4:
                    wait(act, w1_in, 16 * (E + 1))
                    wait(act, g1_done, 8 * E - 8)
                    c, hh = divmod(k, 2)
                    at = slice(hh * 512, hh * 512 + 512)
                    dst, src = W1h[:, par, c, at], W1raw[:, c, at]
                else:
                    wait(act, w2_in, 16 * (E + 1))
                    wait(act, g2_done, 8 * E - 8)
                    at = slice(2 * (k - 4), 2 * (k - 4) + 2)
                    dst, src = W2h[:, par, at], W2raw[:, at]
                nc.scalar.activation(dst, src, ACT.Copy).then_inc(whi, 1)

            def norm(E, par, e, b, J):
                wait(act, st_done, J + 1)
                wait(act, xlo, 2 * E + b - 1)
                at = XT[:, e, :, b] if isinstance(e, int) else XT[:, bass.ds(e, 1), :, b]
                nc.scalar.activation(XN[:, b], at, ACT.Identity, bias=ST[:, NPAIR, B + b:B + b + 1],
                                     scale=ST[:, NPAIR, b:b + 1]).then_inc(xn_done, 1)
                wait(act, xn_done, 2 * E + b + 1)
                wait(act, g1_done, 8 * E - 8)
                nc.scalar.activation(Xh[:, par, :, b], XN[:, b], ACT.Copy).then_inc(xhi, 1)

            def gelu(E, t, func, col):
                s = 8 * E + t
                wait(act, g1_done, s + 1)
                wait(act, hlo, s - 1)
                nc.scalar.activation(HR[:, t % 2], G1[t % 2][:], func, bias=BT[:, bass.ds(col, 1)]
                                     ).then_inc(gelu_done, 1)
                wait(act, gelu_done, s + 1)
                wait(act, g2_done, s - RING + 1)
                nc.scalar.activation(Hh[:, t % RING], HR[:, t % 2], ACT.Copy).then_inc(hhi, 1)

            def out_evac_step(E, b):
                n = E - 2 * C
                wait(act, out_tr, 2 * n + b + 1)
                wait(act, out_st[b], 16 * n)
                nc.scalar.activation(OUTT[:, b].rearrange("p c d -> p (c d)"), TR[:], ACT.Copy
                                     ).then_inc(out_evac, 1)

            def pair(P, f, func, last=False, last_of_all=False):
                for ee in range(2):
                    E, e = 2 * P + ee, 2 * (P - NPAIR * f) + ee
                    J = job_of(P, 0, f == 0) if ee else job_here(P, f)
                    for t in range(HT):
                        gelu(E, t, func, BCOLS * f + HT * e + t)
                        if not (last_of_all and ee):
                            w_hi(E + 1, 1 - ee, t)
                        if t in (2, 4) and not (last and ee):
                            norm(E + 1, 1 - ee, next_e(P, f, ee), t // 2 - 1, J)
                        if f == 2 and t in (5, 7):
                            if not isinstance(P, int) or E > 2 * C:
                                out_evac_step(E - 1, (t - 5) // 2)

            def next_e(P, f, ee):
                e = 2 * (P - NPAIR * f) + ee + 1
                return e % C if isinstance(e, int) else e

            def job_here(P, f):
                if isinstance(P, int):
                    return 0 if P == 0 else 2 * NPAIR if P == NPAIR else job_of(P - 1, 0, f == 0)
                return P if f == 0 else P + 4

            for k in range(8):
                w_hi(0, 0, k)
            for b in range(B):
                norm(0, 0, 0, b, 0)
            act.wait_ge(bias_t, 1)
            pair(0, 0, ACT.Gelu_apprx_tanh)
            with act.Fori(1, 3) as P:
                pair(P, 0, ACT.Gelu_apprx_tanh)
            pair(3, 0, ACT.Gelu_apprx_tanh, last=True)

            def conv_hi(k, i):
                wait(act, cn_done, k + 1)
                wait(act, conv_mm, k - RING + 1)
                nc.scalar.activation(Ch[:, i], CN[:, i % 2], ACT.Copy).then_inc(chi, 1)

            def conv_scale(k, i):
                wait(act, conv_mm, k + 1)
                nc.scalar.activation(ROT[i][:], ROT[i][:], ACT.Identity, bias=conv_bias[:, 0:1],
                                     scale=conv_mean[:, 0:1]).then_inc(cscaled, 1)

            act.wait_ge(prep, 4 + KS)
            for k in range(RING):
                conv_hi(k, k)
                if k >= 2:
                    conv_scale(k - 2, k - 2)
            with act.Fori(RING, NBLK - NBLK % RING, RING) as k:
                for i in range(RING):
                    conv_hi(k + i, i)
                    conv_scale(k + i - 2, (i - 2) % RING)
            for k in range(NBLK - NBLK % RING, NBLK + 2):
                if k < NBLK:
                    conv_hi(k, k % RING)
                conv_scale(k - 2, (k - 2) % RING)

            for b in range(B):
                norm(C, 0, 0, b, 2 * NPAIR)
            pair(4, 1, ACT.Gelu_apprx_tanh)
            with act.Fori(5, 7) as P:
                pair(P, 1, ACT.Gelu_apprx_tanh)
            pair(7, 1, ACT.Gelu_apprx_tanh)
            pair(8, 2, ACT.Gelu)
            with act.Fori(9, 11) as P:
                pair(P, 2, ACT.Gelu)
            pair(11, 2, ACT.Gelu, last=True, last_of_all=True)
            for b in range(B):
                out_evac_step(3 * C - 1, b)

        @block.vector
        def _(dve):
            for i in range(1, B * C, 2):
                e, b = divmod(i, B)
                dve.wait_ge(in_tr, i + 1)
                nc.vector.tensor_copy(XT[:, e, :, b], ROT[i % 4][:].rearrange("p (c n) -> p c n", c=DC)
                                      ).then_inc(in_evac_dve, 1)

            def stats_a(J, e):
                for b in range(B):
                    for i in range(2):
                        at = XT[:, e + i, :, b] if isinstance(e, int) else XT[:, bass.ds(e + i, 1), :, b]
                        nc.vector.bn_stats(BN[:, b, i], at).then_inc(bn_done, 1)

            def stats_aggregate(J):
                for b in range(B):
                    nc.vector.bn_aggr(MV[:, b], BN[:, b].rearrange("p i s -> p (i s)")).then_inc(mv_done, 1)

            def stats_b(J):
                wait(dve, mean_mm, J + 1)
                nc.vector.tensor_copy(MEAN[:], STAT[:, 0:B])
                nc.vector.tensor_tensor(DM[:], MV[:, :, 0], STAT[:, 0:B], ALU.subtract).then_inc(dm_done, 1)
                wait(dve, dm_done, J + 1)
                for b in range(B):
                    nc.vector.scalar_tensor_tensor(Q[:, b:b + 1], DM[:, b:b + 1], DM[:, b:b + 1], MV[:, b, 1:2],
                                                   ALU.mult, ALU.add).then_inc(q_done, 1)

            def stats_c(J):
                wait(dve, var_mm, J + 1)
                nc.vector.tensor_scalar(VE[:], STAT[:, B:2 * B], GN_EPS, None, ALU.add).then_inc(ve_done, 1)

            def stats_d(J, slot):
                wait(dve, rs_done, J + 1)
                at = slice(slot, slot + 1) if isinstance(slot, int) else bass.ds(slot, 1)
                nc.vector.tensor_copy(ST[:, at, 0:B], RS[:].unsqueeze(1))
                nc.vector.scalar_tensor_tensor(ST[:, at, B:2 * B], MEAN[:].unsqueeze(1), -1.0,
                                               RS[:].unsqueeze(1), ALU.mult, ALU.mult).then_inc(st_done, 1)

            def w_lo(E, par, k):
                wait(dve, whi, 8 * E + k + 1)
                if k < 4:
                    c, hh = divmod(k, 2)
                    at = slice(hh * 512, hh * 512 + 512)
                    dst, src, high = W1l[:, par, c, at], W1raw[:, c, at], W1h[:, par, c, at]
                else:
                    at = slice(2 * (k - 4), 2 * (k - 4) + 2)
                    dst, src, high = W2l[:, par, at], W2raw[:, at], W2h[:, par, at]
                nc.vector.tensor_tensor(dst, src, high.bitcast(F32), ALU.subtract).then_inc(wlo, 1)

            def x_lo(E, par, b):
                wait(dve, xhi, 2 * E + b + 1)
                nc.vector.tensor_tensor(Xl[:, par, :, b], XN[:, b], Xh[:, par, :, b].bitcast(F32), ALU.subtract
                                        ).then_inc(xlo, 1)

            def h_lo(E, t):
                wait(dve, hhi, 8 * E + t + 1)
                nc.vector.tensor_tensor(Hl[:, t % RING], HR[:, t % 2], Hh[:, t % RING].bitcast(F32),
                                        ALU.subtract).then_inc(hlo, 1)

            def evict(E, par, e, f):
                wait(dve, g2_done, 8 * E + 8)
                if f == 2:
                    wait(dve, out_tr, 2 * (E - 2 * C) - 2)
                for m in range(DC):
                    at = XT[:, e, m] if isinstance(e, int) else XT[:, bass.ds(e, 1), m]
                    dst = XFIN[:, par, m] if f == 2 else at
                    nc.vector.scalar_tensor_tensor(
                        dst.rearrange("p b n -> p (b n)") if len(dst.shape) == 3 else
                        dst.rearrange("p o b n -> p (o b n)"),
                        ACC[par][m][:], BT[:, bass.ds(BCOLS * f + C * HT + DC * e + m, 1)],
                        at.rearrange("p b n -> p (b n)") if len(at.shape) == 3 else
                        at.rearrange("p o b n -> p (o b n)"), ALU.add, ALU.add).then_inc(evicted, 1)

            def pair(P, f, first=False, last=False, last_of_all=False):
                for ee in range(2):
                    E, e = 2 * P + ee, 2 * (P - NPAIR * f) + ee
                    J = job_of(P, ee, f == 0)
                    for t in range(HT):
                        if J is not None and t == 2:
                            wait(dve, bn_done, 4 * J + 4)
                        h_lo(E, t)
                        if J is not None and t == 2:
                            stats_aggregate(J)
                        if not (last_of_all and ee):
                            w_lo(E + 1, 1 - ee, t)
                        if t in (2, 4) and not (last and ee):
                            x_lo(E + 1, 1 - ee, t // 2 - 1)
                        if t == 2 and not (first and ee == 0):
                            if isinstance(P, int) and e == 0:
                                evict(E - 1, 1 - ee, C - 1, f - 1)
                            else:
                                evict(E - 1, 1 - ee, e - 1, f)
                        if J is not None:
                            if t == 1:
                                if f == 0 and ee:
                                    src = 2 * P - 2
                                    wait(dve, evicted, 4 * P)
                                else:
                                    src = 2 * (P - NPAIR * f) + 2
                                    src = src % C if isinstance(src, int) else src
                                    if isinstance(P, int) and P == NPAIR:
                                        dve.wait_ge(x2_rest, 16 * (C - 2))
                                    if (P if isinstance(P, int) else 7 * f - 7) >= 7:
                                        wait(dve, evicted, 4 * (P - 3) + 4)
                                stats_a(J, src)
                            if t == 4:
                                stats_b(J)
                            if t == 6:
                                stats_c(J)
                            if t == 7:
                                if not (f == 0 and ee):
                                    wait(dve, xn_done, 2 * (2 * P + 1) + 2)
                                stats_d(J, P - 1 if f == 0 and ee else NPAIR)

            dve.wait_ge(in_evac_act, 2)
            dve.wait_ge(in_evac_dve, 2)
            stats_a(0, 0)
            dve.wait_ge(bn_done, 4 * (0) + 4)
            stats_aggregate(0)
            stats_b(0)
            stats_c(0)
            dve.wait_ge(bias_tr, LAYERS)
            nc.vector.tensor_copy(BT[:], TR[:, 0:LAYERS * BCOLS]).then_inc(bias_t, 1)
            for k in range(8):
                w_lo(0, 0, k)
            stats_d(0, NPAIR)
            for b in range(B):
                x_lo(0, 0, b)
            dve.wait_ge(bias_t, 1)
            pair(0, 0, first=True)

            dve.wait_ge(conv_in, 16 * 3 * C)
            dve.wait_ge(consts, 3 + KS)
            nc.vector.tensor_scalar(conv_neg[:], conv_rep[:], 0.0, None, ALU.is_lt).then_inc(prep, 1)
            nc.vector.scalar_tensor_tensor(conv_abs[:], conv_out[:], -1.0, conv_out[:], ALU.mult, ALU.max,
                                           accum_out=conv_sum[:]).then_inc(prep, 1)
            for kw in range(KS):
                nc.vector.tensor_reduce(mask[:, kw], diag[:, kw].rearrange("p c j -> p j c"), AX.X, ALU.add
                                        ).then_inc(prep, 1)
            dve.wait_ge(prep, 2 + KS)
            nc.vector.scalar_tensor_tensor(conv_sign[:], conv_rep[:], 0.0, conv_neg[:], ALU.is_gt, ALU.subtract
                                           ).then_inc(prep, 1)
            nc.vector.tensor_scalar(conv_mean[:], conv_sum[:], 1.0 / (C * KS * KS), None, ALU.mult).then_inc(prep, 1)
            dve.wait_ge(prep, 4 + KS)
            done = 4 + KS
            sign = conv_sign[:].rearrange("p o (a b) -> p a o b", a=KS)
            for kh in range(KS):
                for kw in range(KS):
                    nc.vector.tensor_tensor(band_tap[:, kw],
                                            sign[:, kh, :, kw:kw + 1].broadcast_to([PART, C, ROWS]),
                                            mask[:, kw:kw + 1, :].broadcast_to([PART, C, ROWS]), ALU.mult
                                            ).then_inc(prep, 1)
                done += KS
                dve.wait_ge(prep, done)
                nc.vector.tensor_tensor(band_sum[:], band_tap[:, 0], band_tap[:, 1], ALU.add).then_inc(prep, 1)
                done += 1
                dve.wait_ge(prep, done)
                nc.vector.tensor_tensor(BAND[:, kh], band_sum[:], band_tap[:, 2], ALU.add).then_inc(prep, 1)
                done += 1
                dve.wait_ge(prep, done)

            with dve.Fori(1, 3) as P:
                pair(P, 0)
            pair(3, 0, last=True)
            evict(C - 1, 1, C - 1, 0)

            def to_partitions(g):
                own = slice(g * PART // NPAIR, (g + 1) * PART // NPAIR)
                dve.wait_ge(st_done, [4, 6, 7, 8][g])
                nc.vector.tensor_copy(CST[own], ST[own, g]).then_inc(cst_done, 1)

            dve.wait_ge(evicted, 2 * C)
            stats_a(7, C - 2)
            dve.wait_ge(bn_done, 4 * (7) + 4)
            stats_aggregate(7)
            for g in range(NPAIR - 1):
                to_partitions(g)
            stats_b(7)
            stats_c(7)
            stats_d(7, NPAIR - 1)
            to_partitions(NPAIR - 1)
            dve.wait_ge(xc_in, 16 * 8 * C)
            nc.vector.tensor_copy(XC[:, :, :, 0:1], XC[:, :, :, 1:2]).then_inc(pads, 1)
            nc.vector.tensor_copy(XC[:, :, :, NP - 1:NP], XC[:, :, :, N:N + 1]).then_inc(pads, 1)

            def conv_lo(k, i):
                wait(dve, chi, k + 1)
                nc.vector.tensor_tensor(Cl[:, i], CN[:, i % 2], Ch[:, i].bitcast(F32), ALU.subtract
                                        ).then_inc(clo, 1)

            def conv_add(k, i):
                wait(dve, cscaled, k + 1)
                at = XC[:, k, :, 1:N + 1] if isinstance(k, int) else XC[:, bass.ds(k, 1), :, 1:N + 1]
                nc.vector.tensor_tensor(at, ROT[i][:].rearrange("p (b n) -> p b n", b=B), at, ALU.add
                                        ).then_inc(cadded, 1)

            for k in range(RING):
                conv_lo(k, k)
                if k >= 2:
                    conv_add(k - 2, k - 2)
            with dve.Fori(RING, NBLK - NBLK % RING, RING) as k:
                for i in range(RING):
                    conv_lo(k + i, i)
                    conv_add(k + i - 2, (i - 2) % RING)
            for k in range(NBLK - NBLK % RING, NBLK + 2):
                if k < NBLK:
                    conv_lo(k, k % RING)
                conv_add(k - 2, (k - 2) % RING)

            dve.wait_ge(x2_first, 32)
            stats_a(2 * NPAIR, 0)
            dve.wait_ge(bn_done, 4 * (2 * NPAIR) + 4)
            stats_aggregate(2 * NPAIR)
            stats_b(2 * NPAIR)
            stats_c(2 * NPAIR)
            stats_d(2 * NPAIR, NPAIR)
            for b in range(B):
                x_lo(C, 0, b)
            pair(4, 1, first=True)
            with dve.Fori(5, 7) as P:
                pair(P, 1)
            pair(7, 1)
            pair(8, 2)
            with dve.Fori(9, 11) as P:
                pair(P, 2)
            pair(11, 2, last=True, last_of_all=True)
            evict(3 * C - 1, 1, C - 1, 2)

        @block.tensor
        def _(pe):
            pe.wait_ge(consts, 3)
            for i in range(B * C):
                e, b = divmod(i, B)
                if i % (2 * B) == 0:
                    pe.wait_ge(x_in[e // 2], 32)
                if i >= 4:
                    pe.wait_ge(in_evac_act if i % 2 == 0 else in_evac_dve, (i - 4) // 2 + 1)
                for c in range(DC):
                    for r in range(NC):
                        at = c * N + r * PART
                        ins = nc.tensor.transpose(ROT[i % 4][:, at:at + PART],
                                                  NAT[:, e // 2, b, e % 2, r, c * PART:(c + 1) * PART], ident[:])
                ins.then_inc(in_tr, 1)
            pe.wait_ge(bias_in, 16 * 2 * LAYERS)
            for f in range(LAYERS):
                nc.tensor.transpose(TR[:, f * BCOLS:(f + 1) * BCOLS], bias_rows[:, f, :], ident[0:BCOLS, 0:BCOLS]
                                    ).then_inc(bias_tr, 1)

            def mean_over_partitions(J):
                wait(pe, mv_done, 2 * J + 2)
                wait(pe, ve_done, J)
                nc.tensor.matmul(STAT[:, 0:B], ones_mean[:], MV[:, :, 0], start=True, stop=True
                                 ).then_inc(mean_mm, 1)

            def variance_over_partitions(J):
                wait(pe, q_done, 2 * J + 2)
                nc.tensor.matmul(STAT[:, B:2 * B], ones_mean[:], Q[:], start=True, stop=True).then_inc(var_mm, 1)

            def g1(E, ee, t):
                wait(pe, gelu_done, 8 * E + t - 1)
                if t == 0:
                    wait(pe, xlo, 2 * E + 2)
                    wait(pe, wlo, 8 * E + 4)
                col = slice(t * PART, (t + 1) * PART)
                parts = [(w, xx, c) for c in range(DC) for w, xx in ((W1l, Xh), (W1h, Xl), (W1h, Xh))]
                for n, (w, xx, c) in enumerate(parts):
                    ins = nc.tensor.matmul(G1[t % 2][:], w[:, ee, c, col], xx[:, ee, c].rearrange("p b n -> p (b n)"),
                                           start=n == 0, stop=n == len(parts) - 1)
                ins.then_inc(g1_done, 1)

            def g2(E, ee, t):
                wait(pe, hhi, 8 * E + t + 1)
                if t == 0:
                    wait(pe, wlo, 8 * E + 8)
                    wait(pe, evicted, 2 * E - 2)
                for m in range(DC):
                    col = slice(m * PART, (m + 1) * PART)
                    nc.tensor.matmul(ACC[ee][m][:], W2l[:, ee, t, col], Hh[:, t % RING], start=t == 0, stop=False)
                    nc.tensor.matmul(ACC[ee][m][:], W2h[:, ee, t, col], Hh[:, t % RING], start=False, stop=False)
                wait(pe, hlo, 8 * E + t + 1)
                for m in range(DC):
                    col = slice(m * PART, (m + 1) * PART)
                    ins = nc.tensor.matmul(ACC[ee][m][:], W2h[:, ee, t, col], Hl[:, t % RING], start=False,
                                           stop=t == HT - 1)
                ins.then_inc(g2_done, 1)

            def out_transpose(E, par, b):
                n = E - 2 * C
                wait(pe, evicted, 2 * E + 2)
                wait(pe, out_evac, 2 * n + b)
                for r in range(NC):
                    for c in range(DC):
                        at = r * D + c * PART
                        ins = nc.tensor.transpose(TR[:, at:at + PART], XFIN[:, par, c, b, r * PART:(r + 1) * PART],
                                                  ident[:])
                ins.then_inc(out_tr, 1)

            def pair(P, conv_layer, first=False, putting_out=False):
                for ee in range(2):
                    E = 2 * P + ee
                    J = job_of(P, ee, conv_layer)
                    for t in range(HT):
                        g1(E, ee, t)
                        if t >= 2:
                            g2(E, ee, t - 2)
                        elif not (first and ee == 0):
                            g2(E - 1, 1 - ee, t + HT - 2)
                        if J is not None and t == 3:
                            mean_over_partitions(J)
                        if J is not None and t == 5:
                            variance_over_partitions(J)
                        if putting_out and t in (4, 6):
                            if not isinstance(P, int) or E > 2 * C:
                                out_transpose(E - 1, 1 - ee, t // 2 - 2)

            def drain(E):
                for t in (HT - 2, HT - 1):
                    g2(E, 1, t)

            mean_over_partitions(0)
            variance_over_partitions(0)
            pair(0, True, first=True)
            with pe.Fori(1, 3) as P:
                pair(P, True)
            pair(3, True)
            drain(C - 1)

            mean_over_partitions(7)
            variance_over_partitions(7)

            def conv(k, i):
                wait(pe, clo, k + 1)
                wait(pe, cadded, k - RING + 1)
                parts = [(xx, kh) for kh in range(KS) for xx in (Cl, Ch)]
                for n, (xx, kh) in enumerate(parts):
                    ins = nc.tensor.matmul(ROT[i][:].rearrange("p (b n) -> p b n", b=B),
                                           BAND[:, kh].rearrange("p o j -> p (o j)"), xx[:, i, :, kh:kh + N],
                                           start=n == 0, stop=n == len(parts) - 1)
                ins.then_inc(conv_mm, 1)

            pe.wait_ge(prep, 4 + KS + KS * (KS + 2))
            for k in range(RING):
                conv(k, k)
            with pe.Fori(RING, NBLK - NBLK % RING, RING) as k:
                for i in range(RING):
                    conv(k + i, i)
            for k in range(NBLK - NBLK % RING, NBLK):
                conv(k, k % RING)

            mean_over_partitions(2 * NPAIR)
            variance_over_partitions(2 * NPAIR)
            pair(4, False, first=True)
            with pe.Fori(5, 8) as P:
                pair(P, False)
            pair(8, False, putting_out=True)
            with pe.Fori(9, 11) as P:
                pair(P, False, putting_out=True)
            pair(11, False, putting_out=True)
            drain(3 * C - 1)
            for b in range(B):
                out_transpose(3 * C - 1, 1, b)


_INS = {"x": (B, C, N, D)}
for _l in ("L0", "L2", "L3"):
    _INS.update({f"{_l}_conv_w1": (C, D, H), f"{_l}_conv_b1": (C, H), f"{_l}_conv_w2": (C, H, D),
                 f"{_l}_conv_b2": (C, D)})
_INS.update({"L1_conv_weight": (C, C, KS, KS), "L1_conv_bias": (C,)})


def kernel(**inputs):
    import numpy as np
    import concourse.bacc as bacc
    from concourse.bass_utils import run_bass_kernel_spmd

    nc = bacc.Bacc("TRN2", target_bir_lowering=False, num_devices=1)
    arrays, t = {}, {}
    for name, shape in _INS.items():
        arrays[f"in_{name}"] = np.ascontiguousarray(inputs[name])
        t[name] = nc.dram_tensor(f"in_{name}", shape, F32, kind="ExternalInput").ap()
    out = nc.dram_tensor("out_x", (B, C, N, D), F32, kind="ExternalOutput").ap()
    layers = ("L0", "L2", "L3")
    build(nc, t["x"], *([t[f"{name}_conv_{p}"] for name in layers] for p in ("w1", "b1", "w2", "b2")),
          t["L1_conv_weight"], t["L1_conv_bias"], out)
    r = run_bass_kernel_spmd(nc, [arrays], core_ids=[0])
    return r.results[0]["out_x"]
```

```python
from contextlib import ExitStack

import concourse.bass as bass
import concourse.mybir as mybir

F32 = mybir.dt.float32
F32R = mybir.dt.float32r
ALU = mybir.AluOpType
ACT = mybir.ActivationFunctionType
AX = mybir.AxisListType

B, C, N, D, H = 2, 8, 256, 256, 1024
PART = 128
DC = D // PART
NC = N // PART
TOK = B * N
HT = H // PART
NPAIR = C // 2
LAYERS = 3
BCOLS = C * HT + C * DC
GN_EPS = 1e-5
RING = 4

KS = 3
ROWS = PART // C
OUTR = ROWS - (KS - 1)
NBLK = -(-D // OUTR)
LASTROW = D + 2 - ROWS
NP = N + 2
DP = D + 2
TILES = -(-NBLK // 2)
CRING = 3
GROUPS = [(-(-PART // OUTR), 6), (16, 8), (NBLK - 1, TILES - 1), (NBLK, TILES - 1)]
STORED = [end for end, tile in GROUPS]


def pieces_back():
    pieces = []
    for k in range(NBLK):
        d, end = OUTR * k, min(OUTR * (k + 1), D)
        j = d - LASTROW + 1 if k == NBLK - 1 else 1
        while d < end:
            c = d // PART
            n = min(end, (c + 1) * PART) - d
            if k not in STORED and pieces and n == OUTR and pieces[-1][3] == OUTR and pieces[-1][4] == c:
                k0, blocks, j0, nj, c, p0 = pieces.pop()
                pieces.append((k0, blocks + 1, j0, nj, c, p0))
            else:
                pieces.append((k, 1, j, n, c, d % PART))
            d, j = d + n, j + n
    return pieces


HALVED = (C - 1, C, C + 1)
CROSSED = (C, C + 1)


def units(E):
    return 2 * HT if isinstance(E, int) and E in HALVED else HT


def order(P):
    if isinstance(P, int) and 2 * P in CROSSED:
        return [(ee, b * HT + t) for b in range(B) for ee in range(2) for t in range(HT)]
    return [(ee, t) for ee in range(2) for t in range(units(2 * P + ee if isinstance(P, int) else None))]


def slots(E, layer=None):
    return HT * (E + sum(E > h for h in HALVED)) if isinstance(E, int) else (
        HT * E + (len(HALVED) * HT if layer else 0))


def slot_of(E, t, layer=None):
    if isinstance(E, int) and E in CROSSED:
        return slots(C) + (t // HT * 2 + E - C) * HT + t % HT
    return slots(E, layer) + t


def norm_of(E, b):
    return 2 * C + 2 * b + E - C if isinstance(E, int) and E in CROSSED else 2 * E + b


def evicts(E, layer=None):
    return DC * (E + sum(E > h for h in HALVED)) if isinstance(E, int) else (
        DC * E + (len(HALVED) * DC if layer else 0))


def evicts_for(E, b, layer):
    if not isinstance(E, int):
        return evicts(E - 1, layer)
    if E == C - 1:
        return evicts(E) if b else evicts(E - 1)
    if E in CROSSED:
        return evicts(C) + (2 * b + E - C - 1) * DC if b or E > C else evicts(C)
    return evicts(E) - DC if E == C + 2 else evicts(E - 1)


ONE_BATCH = {7: 0, 8: 1, 9: 0, 10: 1}


def batches(J):
    return (ONE_BATCH[J],) if isinstance(J, int) and J in ONE_BATCH else tuple(range(B))


def jobs_weighed(J, late):
    return B * J - sum(J > j for j in ONE_BATCH) if isinstance(J, int) else B * J - (len(ONE_BATCH) if late else 0)


USUAL = dict(sums=0, aggregate=1, mean=3, deviate=3, variance=5, eps=6, scale=7)


def jobs_of(P, ee, f):
    if not isinstance(P, int):
        if f == 0:
            return [(2 * P + ee, USUAL, 2 * P - 2 if ee else 2 * P + 2, P - 1 if ee else NPAIR)]
        return [] if ee else [(P + 7, USUAL, 2 * (P - NPAIR * f) + 2, NPAIR)]
    E = 2 * P + ee
    if E == 0:
        return [(1, dict(sums=4, aggregate=5, mean=6, deviate=6, variance=7), 2, NPAIR)]
    if E == 1:
        return [(1, dict(eps=0, scale=1), 2, NPAIR)]
    if E == 7:
        return [(6, USUAL, 4, 2),
                (7, dict(sums=10, aggregate=11, mean=12, deviate=12, variance=13, eps=13, scale=14), 6, 3)]
    if E == C:
        return [(11, dict(mean=8, deviate=8, variance=10, eps=10, scale=12), 2, NPAIR)]
    if E == C + 1:
        return [(10, dict(sums=0, aggregate=0, mean=2, deviate=2, variance=3, eps=4, scale=4), 0, NPAIR),
                (11, dict(sums=6, aggregate=7), 2, NPAIR)]
    if P >= 5 and ee == 0 and P + 1 < LAYERS * NPAIR:
        return [(P + 7, USUAL, (2 * P + 2) % C, NPAIR)]
    return []


def job_for(P, f):
    if isinstance(P, int):
        return {0: 0, 1: 1, 2: 2, 3: 4, 4: 10}.get(P, P + 6)
    return P if f == 0 else P + 6


def known(value):
    return value if isinstance(value, int) else -1


def norms_of(P, ee, f):
    E = 2 * P + ee
    if isinstance(P, int) and E in HALVED:
        return {C - 1: {}, C: {4: (C + 1, 0, 9), 10: (C + 1, 1, 10), 13: (C + 2, 0, 11)},
                C + 1: {5: (C, 1, 10), 9: (C + 2, 1, 11)}}[E]
    if isinstance(P, int) and E == LAYERS * C - 1:
        return {}
    if ee and f == 0 and not isinstance(P, int):
        J = 2 * P
    else:
        J = job_for(P + 1 if ee else P, f)
    return {2: (E + 1, 0, J), 4: (E + 1, 1, J)}


def split_at(P, ee, t):
    E = 2 * P + ee
    if isinstance(P, int):
        if E == LAYERS * C - 1:
            return None
        if E == C:
            return t + 4 if t < 4 else None
        if E == C + 1:
            return t - HT if t >= HT else None
    return t if t < HT else None


def build(nc, x, w1, b1, w2, b2, cw, cb, out):
    x1_dram = nc.dram_tensor("x1_scratch", (C, DP, TOK), F32, kind="Internal").ap()
    x2_dram = nc.dram_tensor("x2_scratch", (B, NBLK, ROWS, C, N), F32, kind="Internal").ap()

    with ExitStack() as ctx:
        def sb(name, shape, dt=F32, where=ctx):
            return where.enter_context(nc.sbuf_tensor(name, shape, dt))

        def bank(name):
            return ctx.enter_context(nc.psum_tensor(name, [PART, 512], F32))

        def sem(name):
            return ctx.enter_context(nc.semaphore(name))

        XT = sb("XT", [PART, DC, B, C, N])
        W1raw = sb("W1raw", [PART, DC, H])
        W2raw = sb("W2raw", [PART, HT, D])
        W1h = sb("W1h", [PART, 2, DC, H], F32R)
        W1l = sb("W1l", [PART, 2, DC, H], F32R)
        W2h = sb("W2h", [PART, 2, HT, D], F32R)
        W2l = sb("W2l", [PART, 2, HT, D], F32R)
        XN = sb("XN", [PART, B, DC, N])
        Xh = sb("Xh", [PART, 2, DC, B, N], F32R)
        Xl = sb("Xl", [PART, 2, DC, B, N], F32R)
        ident = sb("ident", [PART, PART])
        ones_mean = sb("ones_mean", [PART, PART])
        half = sb("half", [PART, B])
        gelu_table = sb("gelu_table", [PART, B])
        bias_rows = sb("bias_rows", [BCOLS, LAYERS, PART])
        BT = sb("BT", [PART, LAYERS * BCOLS])
        BN = sb("BN", [PART, B, 2, 6])
        MV = sb("MV", [PART, B, 2])
        MEAN = sb("MEAN", [PART, B])
        DM = sb("DM", [PART, B])
        Q = sb("Q", [PART, B])
        VE = sb("VE", [PART, B])
        RS = sb("RS", [PART, B])
        ST = sb("ST", [PART, NPAIR + 1, 2 * B])
        CST = sb("CST", [PART, 2 * B])
        conv_rep = sb("conv_rep", [PART, C, KS * KS])
        conv_out = sb("conv_out", [PART, C * KS * KS])
        conv_bias = sb("conv_bias", [PART, 1])
        conv_mean = sb("conv_mean", [PART, 1])
        conv_abs = sb("conv_abs", [PART, C * KS * KS])
        conv_sum = sb("conv_sum", [PART, 1])
        conv_neg = sb("conv_neg", [PART, C, KS * KS])
        conv_sign = sb("conv_sign", [PART, C, KS * KS])
        diag = sb("diag", [PART, KS, C, ROWS])
        mask = sb("mask", [PART, KS, ROWS])
        band_tap = sb("band_tap", [PART, KS, C, ROWS])
        band_sum = sb("band_sum", [PART, C, ROWS])
        BAND = sb("BAND", [PART, KS, C, ROWS], F32R)

        CN = sb("CN", [PART, 2, 2, NP])

        with ExitStack() as use:
            NAT = sb("NAT", [PART, NPAIR, B, 2, NC, D], F32, use)
        with ExitStack() as use:
            XFIN = sb("XFIN", [PART, 2, DC, B, N], F32, use)
            OUTT = sb("OUTT", [PART, B, NC, D], F32, use)
        XC = sb("XC", [PART, B, NBLK, NP])

        HR = sb("HR", [PART, 2, TOK])
        with ExitStack() as use:
            Ch = sb("Ch", [PART, CRING, 2, NP], F32R, use)
            Cl = sb("Cl", [PART, CRING, 2, NP], F32R, use)
        Hh = sb("Hh", [PART, RING, TOK], F32R)
        Hl = sb("Hl", [PART, RING, TOK], F32R)

        G1 = [bank(f"G1_{i}") for i in range(2)]
        ACC = [[bank(f"ACC_{i}_{m}") for m in range(DC)] for i in range(2)]
        STAT = bank("STAT")
        TR = bank("TR")
        ROT = [ACC[1][0], ACC[1][1], ACC[0][0], ACC[0][1]]

        x_in = [sem(f"x_in{g}") for g in range(NPAIR)]
        w1_in, w2_in, bias_in, conv_in = sem("w1_in"), sem("w2_in"), sem("bias_in"), sem("conv_in")
        consts, diag_zero = sem("consts"), sem("diag_zero")
        in_tr, in_evac_act, in_evac_dve = sem("in_tr"), sem("in_evac_act"), sem("in_evac_dve")
        bias_tr, bias_t = sem("bias_tr"), sem("bias_t")
        bn_done, mv_done, mean_mm, dm_done = sem("bn_done"), sem("mv_done"), sem("mean_mm"), sem("dm_done")
        q_done, var_mm, ve_done, rs_done, st_done = (sem("q_done"), sem("var_mm"), sem("ve_done"), sem("rs_done"),
                                                     sem("st_done"))
        whi, wlo = sem("whi"), sem("wlo")
        xn_done, xhi, xlo = sem("xn_done"), sem("xhi"), sem("xlo")
        g1_done, gelu_done, hhi, hlo, g2_done = (sem("g1_done"), sem("gelu_done"), sem("hhi"), sem("hlo"),
                                                 sem("g2_done"))
        evicted = sem("evicted")
        prep = sem("prep")
        x1_out, xc_in = sem("x1_out"), sem("xc_in")
        x1_last = [sem(f"x1_last{b}") for b in range(B)]
        xc_last = [sem(f"xc_last{b}") for b in range(B)]
        cst_done, pads = sem("cst_done"), sem("pads")
        cn_done, chi, clo, conv_mm, cscaled, cadded = (sem("cn_done"), sem("chi"), sem("clo"), sem("conv_mm"),
                                                       sem("cscaled"), sem("cadded"))
        x2_out = [[sem(f"x2_out{b}_{n}") for n in range(len(STORED))] for b in range(B)]
        x2_in = [sem(f"x2_in{b}") for b in range(B)]
        out_tr, out_evac = sem("out_tr"), sem("out_evac")
        out_st = [sem(f"out_st{b}") for b in range(B)]

        block = ctx.enter_context(nc.Block())

        def wait(eng, s, value):
            if not isinstance(value, int) or value > 0:
                eng.wait_ge(s, value)

        def acc(E, ee, b):
            return ACC[(ee + b) % 2 if known(E) == C - 1 else ee]

        def batch_of(E, t):
            return t // HT if units(E) > HT else None

        def width(b):
            return TOK if b is None else N

        def evacuated(i):
            return (in_evac_dve, i // 2 - 2) if i % 2 == 0 else (in_evac_act, i // 2 + 3)

        @block.sync
        def _(sp):
            def load_x(g):
                for b in range(B):
                    sp.dma_start(NAT[:, g, b], x[b, 2 * g:2 * g + 2].rearrange("e (c p) d -> p e c d", p=PART)
                                 ).then_inc(x_in[g], 16)

            def load_w1(f, e, E):
                wait(sp, wlo, 8 * E - 4)
                sp.dma_start(W1raw[:], w1[f][e].rearrange("(c p) h -> p c h", p=PART)).then_inc(w1_in, 16)

            def load_w2(f, e, E):
                wait(sp, wlo, 8 * E)
                sp.dma_start(W2raw[:], w2[f][e].rearrange("(t p) d -> p t d", p=PART)).then_inc(w2_in, 16)

            load_x(0)
            load_w1(0, 0, 0)
            for f in range(LAYERS):
                sp.dma_start(bias_rows[0:C * HT, f, :], b1[f].rearrange("e (t p) -> (e t) p", p=PART)
                             ).then_inc(bias_in, 16)
                sp.dma_start(bias_rows[C * HT:BCOLS, f, :], b2[f].rearrange("e (c p) -> (e c) p", p=PART)
                             ).then_inc(bias_in, 16)
            load_w2(0, 0, 0)
            load_x(1)
            load_w1(0, 1, 1)
            for i in range(C):
                sp.dma_start(conv_rep[i * ROWS:(i + 1) * ROWS], cw[:, i].rearrange("o a b -> o (a b)").unsqueeze(0)
                             .broadcast_to([ROWS, C, KS * KS])).then_inc(conv_in, 16)
            sp.dma_start(conv_out[:], cw.rearrange("o i a b -> o (i a b)").unsqueeze(1)
                         .broadcast_to([C, ROWS, C * KS * KS])).then_inc(conv_in, 16)
            sp.dma_start(conv_bias[:], cb.unsqueeze(1).unsqueeze(2).broadcast_to([C, ROWS, 1])
                         ).then_inc(conv_in, 16)
            load_x(2)
            load_w2(0, 1, 1)
            load_x(3)

            def store_x1(e, bs, done):
                sp.wait_ge(evicted, evicts(e + 1) - (DC if bs == (0,) else 0))
                cols = slice(bs[0] * N, (bs[-1] + 1) * N)
                rows = x1_dram[e, :, cols].rearrange("r (b n) -> r b n", n=N)
                for i, b in enumerate(bs):
                    sp.dma_start(rows[1:D + 1, i].rearrange("(c p) n -> p c n", p=PART), XT[:, :, b, e]
                                 ).then_inc(done, 16)
                sp.dma_start(rows[0:1], XT[0:1, 0, bs[0]:bs[-1] + 1, e]).then_inc(done, 16)
                sp.dma_start(rows[D + 1:DP], XT[PART - 1:PART, DC - 1, bs[0]:bs[-1] + 1, e]).then_inc(done, 16)

            def load_xc(e, bs, stored, value, done):
                if e == 0:
                    sp.wait_ge(in_tr, B * C)
                sp.wait_ge(stored, value)
                lo, mid, hi = e * ROWS, e * ROWS + OUTR, (e + 1) * ROWS
                last = NBLK - 1
                for b in bs:
                    rows = x1_dram[e, :, b * N:(b + 1) * N]
                    sp.dma_start(XC[lo:mid, b, 0:last, 1:N + 1],
                                 rows[0:OUTR * last].rearrange("(k j) n -> j k n", j=OUTR)).then_inc(done, 16)
                    sp.dma_start(XC[mid:hi, b, 0:last - 1, 1:N + 1],
                                 rows[OUTR:OUTR * last].rearrange("(k j) n -> j k n", j=OUTR)[0:KS - 1]
                                 ).then_inc(done, 16)
                    sp.dma_start(XC[mid:hi, b, last - 1, 1:N + 1], rows[OUTR * last:OUTR * last + KS - 1]
                                 ).then_inc(done, 16)
                    sp.dma_start(XC[lo:hi, b, last, 1:N + 1], rows[LASTROW:DP]).then_inc(done, 16)

            for E in range(2, C + 1):
                f, e = divmod(E, C)
                if E >= 3:
                    store_x1(E - 3, (0, 1), x1_out)
                load_w1(f, e, E)
                if E >= 3:
                    load_xc(E - 3, (0, 1), x1_out, 64 * (E - 2), xc_in)
                load_w2(f, e, E)
            store_x1(C - 2, (0, 1), x1_out)
            load_xc(C - 2, (0, 1), x1_out, 64 * (C - 1), xc_in)
            for b in range(B):
                store_x1(C - 1, (b,), x1_last[b])
                load_xc(C - 1, (b,), x1_last[b], 48, xc_last[b])
                if b == 0:
                    load_w1(1, 1, C + 1)
                    load_w2(1, 1, C + 1)

            def read_x2(b, n):
                sp.wait_ge(x2_out[b][n], 16 * (STORED[n] - (STORED[n - 1] if n else 0)))
                for k, blocks, j, nj, c, p0 in pieces_back():
                    if k < STORED[n] and (n == 0 or k >= STORED[n - 1]):
                        sp.dma_start(XT[p0:p0 + blocks * nj, c, b],
                                     x2_dram[b, k:k + blocks, j:j + nj].rearrange("k j o n -> k j (o n)")
                                     ).then_inc(x2_in[b], 16)

            for b in range(B):
                for i in range(TILES):
                    sp.wait_ge(cadded, b * TILES + i + 1)
                    for k in range(2 * i, min(2 * i + 2, NBLK)):
                        n = sum(k >= end for end in STORED)
                        sp.dma_start(x2_dram[b, k].rearrange("j o n -> o j n"), XC[:, b, k, 1:N + 1]
                                     ).then_inc(x2_out[b][n], 16)
                    for n, (end, tile) in enumerate(GROUPS):
                        if i == tile:
                            read_x2(b, n)
            with sp.Fori(2, C) as e:
                load_w1(1, e, C + e)
                load_w2(1, e, C + e)

            def store_out(e, b, n):
                wait(sp, out_evac, 2 * n - 1 + b)
                sp.dma_start(out[b, e].rearrange("(c p) d -> p c d", p=PART), OUTT[:, b]).then_inc(out_st[b], 16)

            with sp.Fori(0, 3) as e:
                load_w1(2, e, 2 * C + e)
                load_w2(2, e, 2 * C + e)
            with sp.Fori(3, C) as e:
                load_w1(2, e, 2 * C + e)
                store_out(e - 3, 0, e - 2)
                load_w2(2, e, 2 * C + e)
                store_out(e - 3, 1, e - 2)
            for e in range(C - 3, C):
                for b in range(B):
                    store_out(e, b, e + 1)
            for b in range(B):
                sp.wait_ge(out_st[b], 16 * C)

        @block.gpsimd
        def _(pool):
            nc.gpsimd.memset(ident[:], 0.0).then_inc(diag_zero, 1)
            nc.gpsimd.memset(ones_mean[:], 1.0 / PART).then_inc(consts, 1)
            nc.gpsimd.memset(half[:], -0.5).then_inc(consts, 1)
            nc.gpsimd.memset(diag[:], 0.0).then_inc(diag_zero, 1)
            pool.wait_ge(diag_zero, 1)
            nc.gpsimd.affine_select(out=ident[:], in_=ident[:], compare_op=ALU.not_equal, fill=1.0, base=0,
                                    pattern=[[-1, PART]], channel_multiplier=1).then_inc(consts, 1)
            pool.wait_ge(diag_zero, 2)
            for kw in range(KS):
                nc.gpsimd.affine_select(out=diag[:, kw], in_=diag[:, kw], compare_op=ALU.not_equal, fill=1.0,
                                        base=1 - kw, pattern=[[-ROWS, C], [-1, ROWS]], channel_multiplier=1
                                        ).then_inc(consts, 1)

            def rstd(J, bs=slice(0, B)):
                wait(pool, ve_done, J + 1)
                nc.gpsimd.tensor_tensor(RS[:, bs], VE[:, bs], half[:, bs], ALU.pow).then_inc(rs_done, 1)

            def normalise_tile(q):
                b, i = divmod(q, TILES)
                own = slice(2 * i, min(2 * i + 2, NBLK))
                wait(pool, clo, q - 1)
                nc.gpsimd.tensor_scalar(CN[:, q % 2, 0:own.stop - own.start], XC[:, b, own], CST[:, b:b + 1],
                                        CST[:, B + b:B + b + 1], ALU.mult, ALU.add).then_inc(cn_done, 1)

            with pool.Fori(0, 7) as J:
                rstd(J)
            rstd(7, slice(0, 1))
            for q in range(B * TILES):
                if q % TILES == 0:
                    pool.wait_ge(cst_done, NPAIR + q // TILES)
                    pool.wait_ge(pads, 2 + 2 * (q // TILES))
                normalise_tile(q)
                if q == 7:
                    rstd(8, slice(1, 2))
                if q == 18:
                    rstd(9, slice(0, 1))
            rstd(10, slice(1, 2))
            with pool.Fori(11, 3 + 4 * NPAIR - 1) as J:
                rstd(J)

        @block.scalar
        def _(act):
            def x_evac(i):
                e, b = divmod(i, B)
                act.wait_ge(in_tr, i + 1)
                if i < 4:
                    act.wait_ge(bn_done, i + 1)
                src = ROT[i] if i < 4 else TR
                nc.scalar.activation(XT[:, :, b, e], src[:].rearrange("p (c n) -> p c n", c=DC), ACT.Copy
                                     ).then_inc(in_evac_act, 1)

            def w_hi(E, par, k, layer):
                if k < 4:
                    wait(act, w1_in, 16 * (E + 1))
                    wait(act, g1_done, slots(E - 1, layer) if known(E) != C + 2 else slots(E) - HT)
                    c, hh = divmod(k, 2)
                    at = slice(hh * 512, hh * 512 + 512)
                    dst, src = W1h[:, par, c, at], W1raw[:, c, at]
                else:
                    wait(act, w2_in, 16 * (E + 1))
                    wait(act, g2_done, slots(E - 1, layer) if known(E) != C + 2 else slots(E) - HT)
                    at = slice(2 * (k - 4), 2 * (k - 4) + 2)
                    dst, src = W2h[:, par, at], W2raw[:, at]
                nc.scalar.activation(dst, src, ACT.Copy).then_inc(whi, 1)

            def norm(E, par, e, b, J, layer):
                wait(act, st_done, J + 1)
                m = norm_of(E, b)
                wait(act, xlo, m if known(E) == C + 1 else m - 1)
                at = XT[:, :, b, e] if isinstance(e, int) else XT[:, :, b, bass.ds(e, 1)]
                nc.scalar.activation(XN[:, b], at, ACT.Identity, bias=ST[:, NPAIR, B + b:B + b + 1],
                                     scale=ST[:, NPAIR, b:b + 1]).then_inc(xn_done, 1)
                wait(act, xn_done, m + 1)
                wait(act, g1_done, slots(E - 1, layer) if known(E) != C + 2 else slot_of(C, (b + 1) * HT - 1) + 1)
                nc.scalar.activation(Xh[:, par, :, b], XN[:, b], ACT.Copy).then_inc(xhi, 1)

            def gelu(E, t, func, col, layer):
                s, n = slot_of(E, t, layer), width(batch_of(E, t))
                wait(act, g1_done, s + 1)
                wait(act, hlo, s - 1)
                nc.scalar.activation(HR[:, t % 2, 0:n], G1[t % 2][:, 0:n], func, bias=BT[:, bass.ds(col, 1)]
                                     ).then_inc(gelu_done, 1)
                wait(act, gelu_done, s + 1)
                wait(act, g2_done, s - RING + 1)
                nc.scalar.activation(Hh[:, t % RING, 0:n], HR[:, t % 2, 0:n], ACT.Copy).then_inc(hhi, 1)

            def out_evac_step(E, b):
                n = E - 2 * C
                wait(act, out_tr, 2 * n + b + 1)
                wait(act, out_st[b], 16 * n)
                nc.scalar.activation(OUTT[:, b].rearrange("p c d -> p (c d)"), TR[:], ACT.Copy
                                     ).then_inc(out_evac, 1)

            def pair(P, f, func):
                for ee, t in order(P):
                    E, e = 2 * P + ee, 2 * (P - NPAIR * f) + ee
                    norms = norms_of(P, ee, f)
                    gelu(E, t, func, BCOLS * f + HT * e + t % HT, f)
                    k = split_at(P, ee, t)
                    if k is not None:
                        w_hi(E + 1, 1 - ee, k, f)
                    if t in norms:
                        En, b, J = norms[t]
                        en = En % C if isinstance(En, int) else e + 1
                        norm(En, En % 2 if isinstance(En, int) else 1 - ee, en, b, J, f)
                    if known(E) == 0 and t in (0, 2):
                        x_evac(4 + t)
                    if known(E) == 1 and t % 2 == 0:
                        x_evac(8 + t)
                    if f == 2 and t in (5, 7):
                        if not isinstance(P, int) or E > 2 * C:
                            out_evac_step(E - 1, (t - 5) // 2)

            act.wait_ge(consts, 2)
            nc.scalar.activation(gelu_table[:], half[:], ACT.Gelu_apprx_tanh)
            for i in range(4):
                x_evac(i)
            for k in range(4):
                w_hi(0, 0, k, 0)
            for b in range(B):
                norm(0, 0, 0, b, 0, 0)
            for k in range(4, 8):
                w_hi(0, 0, k, 0)
            act.wait_ge(bias_t, 1)
            pair(0, 0, ACT.Gelu_apprx_tanh)
            with act.Fori(1, 3) as P:
                pair(P, 0, ACT.Gelu_apprx_tanh)
            pair(3, 0, ACT.Gelu_apprx_tanh)

            act.wait_ge(prep, 4 + KS)
            act.wait_ge(g2_done, slots(C))
            for q in range(B * TILES + 2):
                if q < B * TILES:
                    w = 1 if q % TILES == TILES - 1 else 2
                    wait(act, cn_done, q + 1)
                    wait(act, conv_mm, q - CRING + 1)
                    nc.scalar.activation(Ch[:, q % CRING, 0:w], CN[:, q % 2, 0:w], ACT.Copy).then_inc(chi, 1)
                if q >= 2:
                    w = N if (q - 2) % TILES == TILES - 1 else 2 * N
                    wait(act, conv_mm, q - 1)
                    bank_q = ROT[(q - 2) % 4][:, 0:w]
                    nc.scalar.activation(bank_q, bank_q, ACT.Identity, bias=conv_bias[:, 0:1],
                                         scale=conv_mean[:, 0:1]).then_inc(cscaled, 1)
                if q == 20:
                    norm(C, 0, 0, 0, 9, 1)
            for k in range(4):
                w_hi(C + 1, 1, k, 1)

            pair(4, 1, ACT.Gelu_apprx_tanh)
            for P in range(5, 8):
                pair(P, 1, ACT.Gelu_apprx_tanh)
            pair(8, 2, ACT.Gelu)
            with act.Fori(9, 11) as P:
                pair(P, 2, ACT.Gelu)
            pair(11, 2, ACT.Gelu)
            for b in range(B):
                out_evac_step(3 * C - 1, b)

        @block.vector
        def _(dve):
            def x_evac(i):
                e, b = divmod(i, B)
                dve.wait_ge(in_tr, i + 1)
                nc.vector.tensor_copy(XT[:, :, b, e], TR[:].rearrange("p (c n) -> p c n", c=DC)
                                      ).then_inc(in_evac_dve, 1)

            def sums(J, e):
                for b in batches(J):
                    for i in range(2):
                        at = XT[:, :, b, e + i] if isinstance(e, int) else XT[:, :, b, bass.ds(e + i, 1)]
                        nc.vector.bn_stats(BN[:, b, i], at).then_inc(bn_done, 1)

            def sums_done(J, late=False):
                wait(dve, bn_done, 2 * (jobs_weighed(J, late) + len(batches(J))))

            def aggregate(J):
                for b in batches(J):
                    nc.vector.bn_aggr(MV[:, b], BN[:, b].rearrange("p i s -> p (i s)")).then_inc(mv_done, 1)

            def deviate(J):
                bs = batches(J)
                own = slice(bs[0], bs[-1] + 1)
                wait(dve, mean_mm, J + 1)
                nc.vector.tensor_copy(MEAN[:, own], STAT[:, own])
                nc.vector.tensor_tensor(DM[:, own], MV[:, own, 0], STAT[:, own], ALU.subtract).then_inc(dm_done, 1)
                wait(dve, dm_done, J + 1)
                for b in bs:
                    nc.vector.scalar_tensor_tensor(Q[:, b:b + 1], DM[:, b:b + 1], DM[:, b:b + 1], MV[:, b, 1:2],
                                                   ALU.mult, ALU.add).then_inc(q_done, 1)

            def add_eps(J):
                bs = batches(J)
                wait(dve, var_mm, J + 1)
                nc.vector.tensor_scalar(VE[:, bs[0]:bs[-1] + 1], STAT[:, B + bs[0]:B + bs[-1] + 1], GN_EPS, None,
                                        ALU.add).then_inc(ve_done, 1)

            def scale_shift(J, slot):
                bs = batches(J)
                own = slice(bs[0], bs[-1] + 1)
                wait(dve, rs_done, J + 1)
                at = slice(slot, slot + 1) if isinstance(slot, int) else bass.ds(slot, 1)
                nc.vector.tensor_copy(ST[:, at, own], RS[:, own].unsqueeze(1))
                nc.vector.scalar_tensor_tensor(ST[:, at, B + bs[0]:B + bs[-1] + 1], MEAN[:, own].unsqueeze(1), -1.0,
                                               RS[:, own].unsqueeze(1), ALU.mult, ALU.mult).then_inc(st_done, 1)

            def w_lo(E, par, k):
                wait(dve, whi, 8 * E + k + 1)
                if k < 4:
                    c, hh = divmod(k, 2)
                    at = slice(hh * 512, hh * 512 + 512)
                    dst, src, high = W1l[:, par, c, at], W1raw[:, c, at], W1h[:, par, c, at]
                else:
                    at = slice(2 * (k - 4), 2 * (k - 4) + 2)
                    dst, src, high = W2l[:, par, at], W2raw[:, at], W2h[:, par, at]
                nc.vector.tensor_tensor(dst, src, high.bitcast(F32), ALU.subtract).then_inc(wlo, 1)

            def x_lo(E, par, b):
                wait(dve, xhi, norm_of(E, b) + 1)
                nc.vector.tensor_tensor(Xl[:, par, :, b], XN[:, b], Xh[:, par, :, b].bitcast(F32), ALU.subtract
                                        ).then_inc(xlo, 1)

            def h_lo(E, t, layer):
                n = width(batch_of(E, t))
                wait(dve, hhi, slot_of(E, t, layer) + 1)
                nc.vector.tensor_tensor(Hl[:, t % RING, 0:n], HR[:, t % 2, 0:n],
                                        Hh[:, t % RING, 0:n].bitcast(F32), ALU.subtract).then_inc(hlo, 1)

            def evict(E, par, e, f, b=None):
                wait(dve, g2_done, slot_of(E, HT - 1 if b is None else (b + 1) * HT - 1, f) + 1)
                if f == 2:
                    wait(dve, out_tr, 2 * (E - 2 * C) - 2)
                n = width(b)
                for m in range(DC):
                    bs = slice(0, B) if b is None else slice(b, b + 1)
                    at = XT[:, m, bs, e] if isinstance(e, int) else XT[:, m, bs, bass.ds(e, 1)]
                    dst = XFIN[:, par, m] if f == 2 else at
                    nc.vector.scalar_tensor_tensor(
                        dst, acc(E, par, b or 0)[m][:, 0:n].rearrange("p (b n) -> p b n", n=N),
                        BT[:, bass.ds(BCOLS * f + C * HT + DC * e + m, 1)],
                        at, ALU.add, ALU.add).then_inc(evicted, 1)

            def to_partitions(g, b):
                own = slice(g * PART // NPAIR, (g + 1) * PART // NPAIR)
                cols = slice(0, 2 * B) if b is None else slice(b, 2 * B, B)
                nc.vector.tensor_copy(CST[own, cols], ST[own, g, cols]).then_inc(cst_done, 1)

            def double_edges(b):
                dve.wait_ge(xc_in, 16 * 8 * (C - 1))
                dve.wait_ge(xc_last[b], 16 * 4)
                nc.vector.tensor_copy(XC[:, b, :, 0:1], XC[:, b, :, 1:2]).then_inc(pads, 1)
                nc.vector.tensor_copy(XC[:, b, :, NP - 1:NP], XC[:, b, :, N:N + 1]).then_inc(pads, 1)

            def pair(P, f):
                for ee, t in order(P):
                    E, e = 2 * P + ee, 2 * (P - NPAIR * f) + ee
                    jobs, norms = jobs_of(P, ee, f), norms_of(P, ee, f)
                    for J, steps, src, slot in jobs:
                        if steps.get("aggregate") == t and steps["sums"] != t:
                            sums_done(J, f > 0)
                    if known(E) in CROSSED and t % HT == 2:
                        if (ee, t) != (0, 2):
                            evict(E - 1 if ee else E + 1, 1 - ee, 1 - ee, f, t // HT if ee else 0)
                    elif known(E) == C + 2 and t == 2:
                        evict(E - 1, 1, e - 1, f, 1)
                    elif t == 2 and known(E) != 0:
                        if known(E) == 2 * C:
                            evict(E - 1, 1 - ee, C - 1, 1)
                        else:
                            evict(E - 1, 1 - ee, e - 1, f)
                    elif t == HT + 2:
                        evict(E, ee, e, f, 0)
                    h_lo(E, t, f)
                    k = split_at(P, ee, t)
                    if k is not None:
                        w_lo(E + 1, 1 - ee, k)
                    for J, steps, src, slot in jobs:
                        if steps.get("sums") == t:
                            if known(E) == 0:
                                for i in (7, 8):
                                    dve.wait_ge(*evacuated(i))
                            if known(J) == 10:
                                dve.wait_ge(x2_in[1], 16 * len(pieces_back()))
                            if known(J) == 7:
                                dve.wait_ge(evicted, evicts(C) - DC)
                            elif f == 0 and ee:
                                wait(dve, evicted, evicts(2 * P, 0))
                            elif known(P) == 7 or f == 2:
                                wait(dve, evicted, evicts(2 * P - 4, 1))
                            sums(J, src)
                        if steps.get("aggregate") == t:
                            if steps["sums"] == t:
                                sums_done(J, f > 0)
                            aggregate(J)
                        if steps.get("deviate") == t:
                            deviate(J)
                        if steps.get("eps") == t:
                            add_eps(J)
                        if steps.get("scale") == t:
                            if not (f == 0 and ee and known(E) != 1) and known(J) != 10:
                                wait(dve, xn_done, 2 * (2 * P + 1) + 2)
                            scale_shift(J, slot)
                    if t in norms:
                        En, b, J = norms[t]
                        x_lo(En, En % 2 if isinstance(En, int) else 1 - ee, b)
                    if known(E) == 0 and t in (1, 3):
                        x_evac(4 + t)
                    if known(E) == 1 and t % 2 == 1:
                        x_evac(8 + t)
                    if known(E) == C - 1 and t == HT:
                        dve.wait_ge(st_done, 7)
                        for g in range(NPAIR - 1):
                            to_partitions(g, None)
                    if known(E) == C - 1 and t == 14:
                        dve.wait_ge(st_done, 8)
                        to_partitions(NPAIR - 1, 0)

            for i in range(4):
                e, b = divmod(i, B)
                dve.wait_ge(in_tr, i + 1)
                nc.vector.bn_stats(BN[:, b, e], ROT[i][:]).then_inc(bn_done, 1)
            sums_done(0)
            aggregate(0)
            deviate(0)
            w_lo(0, 0, 0)
            add_eps(0)
            w_lo(0, 0, 1)
            scale_shift(0, NPAIR)
            for k in (2, 3):
                w_lo(0, 0, k)
            for b in range(B):
                x_lo(0, 0, b)
            dve.wait_ge(bias_tr, LAYERS)
            nc.vector.tensor_copy(BT[:], TR[:, 0:LAYERS * BCOLS]).then_inc(bias_t, 1)
            for k in range(4, 8):
                w_lo(0, 0, k)
            dve.wait_ge(bias_t, 1)
            pair(0, 0)

            dve.wait_ge(conv_in, 16 * (C + 2))
            dve.wait_ge(consts, 3 + KS)
            nc.vector.tensor_scalar(conv_neg[:], conv_rep[:], 0.0, None, ALU.is_lt).then_inc(prep, 1)
            nc.vector.scalar_tensor_tensor(conv_abs[:], conv_out[:], -1.0, conv_out[:], ALU.mult, ALU.max,
                                           accum_out=conv_sum[:]).then_inc(prep, 1)
            for kw in range(KS):
                nc.vector.tensor_reduce(mask[:, kw], diag[:, kw].rearrange("p c j -> p j c"), AX.X, ALU.add
                                        ).then_inc(prep, 1)
            dve.wait_ge(prep, 2 + KS)
            nc.vector.scalar_tensor_tensor(conv_sign[:], conv_rep[:], 0.0, conv_neg[:], ALU.is_gt, ALU.subtract
                                           ).then_inc(prep, 1)
            nc.vector.tensor_scalar(conv_mean[:], conv_sum[:], 1.0 / (C * KS * KS), None, ALU.mult).then_inc(prep, 1)
            dve.wait_ge(prep, 4 + KS)
            done = 4 + KS
            sign = conv_sign[:].rearrange("p o (a b) -> p a o b", a=KS)
            for kh in range(KS):
                for kw in range(KS):
                    nc.vector.tensor_tensor(band_tap[:, kw],
                                            sign[:, kh, :, kw:kw + 1].broadcast_to([PART, C, ROWS]),
                                            mask[:, kw:kw + 1, :].broadcast_to([PART, C, ROWS]), ALU.mult
                                            ).then_inc(prep, 1)
                done += KS
                dve.wait_ge(prep, done)
                nc.vector.tensor_tensor(band_sum[:], band_tap[:, 0], band_tap[:, 1], ALU.add).then_inc(prep, 1)
                done += 1
                dve.wait_ge(prep, done)
                nc.vector.tensor_tensor(BAND[:, kh], band_sum[:], band_tap[:, 2], ALU.add).then_inc(prep, 1)
                done += 1
                dve.wait_ge(prep, done)

            for i in (B * C - 1, B * C):
                dve.wait_ge(*evacuated(i))
            with dve.Fori(1, 3) as P:
                pair(P, 0)
            pair(3, 0)
            double_edges(0)

            for q in range(B * TILES + 2):
                if q < B * TILES:
                    w = 1 if q % TILES == TILES - 1 else 2
                    wait(dve, chi, q + 1)
                    nc.vector.tensor_tensor(Cl[:, q % CRING, 0:w], CN[:, q % 2, 0:w],
                                            Ch[:, q % CRING, 0:w].bitcast(F32), ALU.subtract).then_inc(clo, 1)
                if q >= 2:
                    b, i = divmod(q - 2, TILES)
                    own = slice(2 * i, min(2 * i + 2, NBLK))
                    w = own.stop - own.start
                    wait(dve, cscaled, q - 1)
                    at = XC[:, b, own, 1:N + 1]
                    nc.vector.tensor_tensor(at, ROT[(q - 2) % 4][:, 0:w * N].rearrange("p (k n) -> p k n", k=w),
                                            at, ALU.add).then_inc(cadded, 1)
                if q == 1:
                    evict(C - 1, 1, C - 1, 0, 1)
                if q == 2:
                    dve.wait_ge(evicted, evicts(C))
                    sums(8, C - 2)
                if q == 3:
                    sums_done(8)
                    aggregate(8)
                if q == 4:
                    deviate(8)
                if q == 6:
                    add_eps(8)
                if q == 8:
                    scale_shift(8, NPAIR - 1)
                    dve.wait_ge(st_done, 9)
                    to_partitions(NPAIR - 1, 1)
                    double_edges(1)
                if q == 16:
                    dve.wait_ge(x2_in[0], 16 * len(pieces_back()))
                    sums(9, 0)
                    sums_done(9)
                    aggregate(9)
                if q == 17:
                    deviate(9)
                if q == 18:
                    add_eps(9)
                    scale_shift(9, NPAIR)
                if q == 21:
                    x_lo(C, 0, 0)
            for k in range(4):
                w_lo(C + 1, 1, k)

            pair(4, 1)
            for P in range(5, 8):
                pair(P, 1)
            pair(8, 2)
            with dve.Fori(9, 11) as P:
                pair(P, 2)
            pair(11, 2)
            evict(3 * C - 1, 1, C - 1, 2)

        @block.tensor
        def _(pe):
            def x_transpose(i):
                e, b = divmod(i, B)
                if i % (2 * B) == 0:
                    pe.wait_ge(x_in[e // 2], 32)
                if i == 4:
                    pe.wait_ge(bias_t, 1)
                if i > 4:
                    pe.wait_ge(*evacuated(i))
                dst = ROT[i] if i < 4 else TR
                for c in range(DC):
                    for r in range(NC):
                        at = c * N + r * PART
                        ins = nc.tensor.transpose(dst[:, at:at + PART],
                                                  NAT[:, e // 2, b, e % 2, r, c * PART:(c + 1) * PART], ident[:])
                ins.then_inc(in_tr, 1)

            def mean_over_partitions(J, late=False):
                bs = batches(J)
                wait(pe, mv_done, jobs_weighed(J, late) + len(bs))
                wait(pe, ve_done, J)
                nc.tensor.matmul(STAT[:, bs[0]:bs[-1] + 1], ones_mean[:], MV[:, bs[0]:bs[-1] + 1, 0], start=True,
                                 stop=True).then_inc(mean_mm, 1)

            def variance_over_partitions(J, late=False):
                bs = batches(J)
                wait(pe, q_done, jobs_weighed(J, late) + len(bs))
                nc.tensor.matmul(STAT[:, B + bs[0]:B + bs[-1] + 1], ones_mean[:], Q[:, bs[0]:bs[-1] + 1], start=True,
                                 stop=True).then_inc(var_mm, 1)

            def g1(E, ee, t, layer):
                b = batch_of(E, t)
                wait(pe, gelu_done, slot_of(E, t, layer) - 1)
                if t % HT == 0:
                    wait(pe, xlo, norm_of(E, B - 1 if b is None else b) + 1)
                    wait(pe, wlo, 8 * E + 4)
                t8 = t % HT
                col = slice(t8 * PART, (t8 + 1) * PART)
                parts = [(w, xx, c) for c in range(DC) for w, xx in ((W1l, Xh), (W1h, Xl), (W1h, Xh))]
                for n, (w, xx, c) in enumerate(parts):
                    rhs = xx[:, ee, c].rearrange("p b n -> p (b n)") if b is None else xx[:, ee, c, b]
                    ins = nc.tensor.matmul(G1[t % 2][:, 0:width(b)], w[:, ee, c, col], rhs,
                                           start=n == 0, stop=n == len(parts) - 1)
                ins.then_inc(g1_done, 1)

            def g2(E, ee, t, layer):
                b = batch_of(E, t)
                n, s, t8 = width(b), slot_of(E, t, layer), t % HT
                banks = acc(E, ee, b or 0)
                wait(pe, hhi, s + 1)
                if t8 == 0:
                    wait(pe, wlo, 8 * E + 8)
                    wait(pe, evicted, evicts_for(E, b, layer))
                for m in range(DC):
                    col = slice(m * PART, (m + 1) * PART)
                    high = Hh[:, t % RING, 0:n]
                    nc.tensor.matmul(banks[m][:, 0:n], W2l[:, ee, t8, col], high, start=t8 == 0, stop=False)
                    nc.tensor.matmul(banks[m][:, 0:n], W2h[:, ee, t8, col], high, start=False, stop=False)
                wait(pe, hlo, s + 1)
                for m in range(DC):
                    col = slice(m * PART, (m + 1) * PART)
                    ins = nc.tensor.matmul(banks[m][:, 0:n], W2h[:, ee, t8, col], Hl[:, t % RING, 0:n],
                                           start=False, stop=t8 == HT - 1)
                ins.then_inc(g2_done, 1)

            def out_transpose(E, par, b):
                n = E - 2 * C
                wait(pe, evicted, evicts(E + 1, 2))
                wait(pe, out_evac, 2 * n + b)
                for r in range(NC):
                    for c in range(DC):
                        at = r * D + c * PART
                        ins = nc.tensor.transpose(TR[:, at:at + PART], XFIN[:, par, c, b, r * PART:(r + 1) * PART],
                                                  ident[:])
                ins.then_inc(out_tr, 1)

            def pair(P, f):
                steps_of_pair = order(P)
                for u, (ee, t) in enumerate(steps_of_pair):
                    E = 2 * P + ee
                    g1(E, ee, t, f)
                    if u >= 2:
                        ee2, t2 = steps_of_pair[u - 2]
                        g2(2 * P + ee2, ee2, t2, f)
                    elif not (known(E) in (0, C)):
                        g2(E - 1, 1, t + units(E - 1) - 2, f)
                    for J, steps, src, slot in jobs_of(P, ee, f):
                        if steps.get("mean") == t:
                            mean_over_partitions(J, f > 0)
                        if steps.get("variance") == t:
                            variance_over_partitions(J, f > 0)
                    if known(E) == 0 and t < 4:
                        x_transpose(4 + t)
                    if known(E) == 1:
                        x_transpose(8 + t)
                    if f == 2 and t in (4, 6) and (not isinstance(P, int) or E > 2 * C):
                        out_transpose(E - 1, 1 - ee, t // 2 - 2)

            def drain(E, f):
                for t in (units(E) - 2, units(E) - 1):
                    g2(E, 1, t, f)

            pe.wait_ge(consts, 3)
            for i in range(4):
                x_transpose(i)
            mean_over_partitions(0)
            variance_over_partitions(0)
            pe.wait_ge(bias_in, 16 * 2 * LAYERS)
            for f in range(LAYERS):
                nc.tensor.transpose(TR[:, f * BCOLS:(f + 1) * BCOLS], bias_rows[:, f, :], ident[0:BCOLS, 0:BCOLS]
                                    ).then_inc(bias_tr, 1)
            pair(0, 0)
            with pe.Fori(1, 3) as P:
                pair(P, 0)
            pair(3, 0)
            drain(C - 1, 0)

            pe.wait_ge(prep, 4 + KS + KS * (KS + 2))
            for q in range(B * TILES):
                w = 1 if q % TILES == TILES - 1 else 2
                if q == 4:
                    mean_over_partitions(8)
                if q == 6:
                    variance_over_partitions(8)
                if q == 17:
                    mean_over_partitions(9)
                if q == 18:
                    variance_over_partitions(9)
                if q == 2:
                    pe.wait_ge(evicted, evicts(C))
                wait(pe, clo, q + 1)
                wait(pe, cadded, q - 3)
                parts = [(xx, kh) for kh in range(KS) for xx in (Cl, Ch)]
                for n, (xx, kh) in enumerate(parts):
                    ins = nc.tensor.matmul(ROT[q % 4][:, 0:w * N].rearrange("p (k n) -> p k n", k=w),
                                           BAND[:, kh].rearrange("p o j -> p (o j)"),
                                           xx[:, q % CRING, 0:w, kh:kh + N], start=n == 0, stop=n == len(parts) - 1)
                ins.then_inc(conv_mm, 1)

            pair(4, 1)
            pair(5, 1)
            with pe.Fori(6, 8) as P:
                pair(P, 1)
            pair(8, 2)
            with pe.Fori(9, 11) as P:
                pair(P, 2)
            pair(11, 2)
            drain(3 * C - 1, 2)
            for b in range(B):
                out_transpose(3 * C - 1, 1, b)


_INS = {"x": (B, C, N, D)}
for _l in ("L0", "L2", "L3"):
    _INS.update({f"{_l}_conv_w1": (C, D, H), f"{_l}_conv_b1": (C, H), f"{_l}_conv_w2": (C, H, D),
                 f"{_l}_conv_b2": (C, D)})
_INS.update({"L1_conv_weight": (C, C, KS, KS), "L1_conv_bias": (C,)})


def kernel(**inputs):
    import numpy as np
    import concourse.bacc as bacc
    from concourse.bass_utils import run_bass_kernel_spmd

    nc = bacc.Bacc("TRN2", target_bir_lowering=False, num_devices=1)
    arrays, t = {}, {}
    for name, shape in _INS.items():
        arrays[f"in_{name}"] = np.ascontiguousarray(inputs[name])
        t[name] = nc.dram_tensor(f"in_{name}", shape, F32, kind="ExternalInput").ap()
    out = nc.dram_tensor("out_x", (B, C, N, D), F32, kind="ExternalOutput").ap()
    layers = ("L0", "L2", "L3")
    build(nc, t["x"], *([t[f"{name}_conv_{p}"] for name in layers] for p in ("w1", "b1", "w2", "b2")),
          t["L1_conv_weight"], t["L1_conv_bias"], out)
    r = run_bass_kernel_spmd(nc, [arrays], core_ids=[0])
    return r.results[0]["out_x"]
```

```python
from contextlib import ExitStack

import concourse.bass as bass
import concourse.mybir as mybir

F32 = mybir.dt.float32
F32R = mybir.dt.float32r
ALU = mybir.AluOpType
ACT = mybir.ActivationFunctionType
AX = mybir.AxisListType

B, C, N, D, H = 2, 8, 256, 256, 1024
PART = 128
DC = D // PART
NC = N // PART
TOK = B * N
HT = H // PART
NPAIR = C // 2
LAYERS = 3
BCOLS = C * HT + C * DC
GN_EPS = 1e-5
RING = 4

KS = 3
ROWS = PART // C
OUTR = ROWS - (KS - 1)
NBLK = -(-D // OUTR)
LASTROW = D + 2 - ROWS
NP = N + 2
DP = D + 2
TILES = -(-NBLK // 2)
CRING = 3
GROUPS = [(6, 5), (10, 7), (16, 9), (NBLK, TILES - 1)]
STORED = [end for end, tile in GROUPS]


def pieces_back():
    pieces = []
    for k in range(NBLK):
        d, end = OUTR * k, min(OUTR * (k + 1), D)
        j = d - LASTROW + 1 if k == NBLK - 1 else 1
        while d < end:
            c = d // PART
            n = min(end, (c + 1) * PART) - d
            if k not in STORED and pieces and n == OUTR and pieces[-1][3] == OUTR and pieces[-1][4] == c:
                k0, blocks, j0, nj, c, p0 = pieces.pop()
                pieces.append((k0, blocks + 1, j0, nj, c, p0))
            else:
                pieces.append((k, 1, j, n, c, d % PART))
            d, j = d + n, j + n
    return pieces


HALVED = (C - 1, C, C + 1)
CROSSED = (C, C + 1)


def units(E):
    return 2 * HT if isinstance(E, int) and E in HALVED else HT


def order(P):
    if isinstance(P, int) and 2 * P in CROSSED:
        return [(ee, b * HT + t) for b in range(B) for ee in range(2) for t in range(HT)]
    return [(ee, t) for ee in range(2) for t in range(units(2 * P + ee if isinstance(P, int) else None))]


def slots(E, layer=None):
    return HT * (E + sum(E > h for h in HALVED)) if isinstance(E, int) else (
        HT * E + (len(HALVED) * HT if layer else 0))


def slot_of(E, t, layer=None):
    if isinstance(E, int) and E in CROSSED:
        return slots(C) + (t // HT * 2 + E - C) * HT + t % HT
    return slots(E, layer) + t


def norm_of(E, b):
    return 2 * C + 2 * b + E - C if isinstance(E, int) and E in CROSSED else 2 * E + b


def evicts(E, layer=None):
    return DC * (E + sum(E > h for h in HALVED)) if isinstance(E, int) else (
        DC * E + (len(HALVED) * DC if layer else 0))


def evicts_for(E, b, layer):
    if not isinstance(E, int):
        return evicts(E - 1, layer)
    if E == C - 1:
        return evicts(E) if b else evicts(E - 1)
    if E in CROSSED:
        return evicts(C) + (2 * b + E - C - 1) * DC if b or E > C else evicts(C)
    return evicts(E) - DC if E == C + 2 else evicts(E - 1)


ONE_BATCH = {7: 0, 8: 1, 9: 0, 10: 1}


def batches(J):
    return (ONE_BATCH[J],) if isinstance(J, int) and J in ONE_BATCH else tuple(range(B))


def jobs_weighed(J, late):
    return B * J - sum(J > j for j in ONE_BATCH) if isinstance(J, int) else B * J - (len(ONE_BATCH) if late else 0)


USUAL = dict(sums=0, aggregate=1, mean=3, deviate=3, variance=5, eps=6, scale=7)


def jobs_of(P, ee, f):
    if not isinstance(P, int):
        if f == 0:
            return [(2 * P + ee, USUAL, 2 * P - 2 if ee else 2 * P + 2, P - 1 if ee else NPAIR)]
        return [] if ee else [(P + 7, USUAL, 2 * (P - NPAIR * f) + 2, NPAIR)]
    E = 2 * P + ee
    if E == 0:
        return [(1, dict(sums=4, aggregate=5, mean=7, deviate=7), 2, NPAIR)]
    if E == 1:
        return [(1, dict(variance=0, eps=0, scale=1), 2, NPAIR)]
    if E == 7:
        return [(6, dict(sums=0, aggregate=1, mean=4, deviate=4, variance=6, eps=7, scale=8), 4, 2),
                (7, dict(sums=10, aggregate=11, mean=12, deviate=12, variance=13, eps=13, scale=14), 6, 3)]
    if E == C:
        return [(11, dict(mean=9, deviate=9, variance=11, eps=11, scale=12), 2, NPAIR)]
    if E == C + 1:
        return [(10, dict(sums=0, aggregate=0, mean=2, deviate=2, variance=3, eps=4, scale=4), 0, NPAIR),
                (11, dict(sums=5, more_sums=6, aggregate=7), 2, NPAIR)]
    if P >= 5 and ee == 0 and P + 1 < LAYERS * NPAIR:
        return [(P + 7, USUAL, (2 * P + 2) % C, NPAIR)]
    return []


def job_for(P, f):
    if isinstance(P, int):
        return {0: 0, 1: 1, 2: 2, 3: 4, 4: 10}.get(P, P + 6)
    return P if f == 0 else P + 6


def known(value):
    return value if isinstance(value, int) else -1


def norms_of(P, ee, f):
    E = 2 * P + ee
    if isinstance(P, int) and E in HALVED:
        return {C - 1: {}, C: {5: (C + 1, 0, 9), 10: (C + 1, 1, 10), 13: (C + 2, 0, 11)},
                C + 1: {5: (C, 1, 10), 9: (C + 2, 1, 11)}}[E]
    if isinstance(P, int) and E == LAYERS * C - 1:
        return {}
    if ee and f == 0 and not isinstance(P, int):
        J = 2 * P
    else:
        J = job_for(P + 1 if ee else P, f)
    return {2: (E + 1, 0, J), 4: (E + 1, 1, J)}


def split_at(P, ee, t):
    E = 2 * P + ee
    if isinstance(P, int):
        if E == LAYERS * C - 1:
            return None
        if E == C:
            return t + 4 if t < 4 else None
        if E == C + 1:
            return t - HT if t >= HT else None
    return t if t < HT else None


def build(nc, x, w1, b1, w2, b2, cw, cb, out):
    x1_dram = nc.dram_tensor("x1_scratch", (C, DP, TOK), F32, kind="Internal").ap()
    x2_dram = nc.dram_tensor("x2_scratch", (B, NBLK, ROWS, C, N), F32, kind="Internal").ap()

    with ExitStack() as ctx:
        def sb(name, shape, dt=F32, where=ctx):
            return where.enter_context(nc.sbuf_tensor(name, shape, dt))

        def bank(name):
            return ctx.enter_context(nc.psum_tensor(name, [PART, 512], F32))

        def sem(name):
            return ctx.enter_context(nc.semaphore(name))

        XT = sb("XT", [PART, DC, B, C, N])
        W1raw = sb("W1raw", [PART, DC, H])
        W2raw = sb("W2raw", [PART, HT, D])
        W1h = sb("W1h", [PART, 2, DC, H], F32R)
        W1l = sb("W1l", [PART, 2, DC, H], F32R)
        W2h = sb("W2h", [PART, 2, HT, D], F32R)
        W2l = sb("W2l", [PART, 2, HT, D], F32R)
        XN = sb("XN", [PART, B, DC, N])
        Xh = sb("Xh", [PART, 2, DC, B, N], F32R)
        Xl = sb("Xl", [PART, 2, DC, B, N], F32R)
        ident = sb("ident", [PART, PART])
        ones_mean = sb("ones_mean", [PART, PART])
        half = sb("half", [PART, B])
        gelu_table = sb("gelu_table", [PART, B])
        bias_rows = sb("bias_rows", [BCOLS, LAYERS, PART])
        BT = sb("BT", [PART, LAYERS * BCOLS])
        BN = sb("BN", [PART, B, 2, 6])
        MV = sb("MV", [PART, B, 2])
        MEAN = sb("MEAN", [PART, B])
        DM = sb("DM", [PART, B])
        Q = sb("Q", [PART, B])
        VE = sb("VE", [PART, B])
        RS = sb("RS", [PART, B])
        ST = sb("ST", [PART, NPAIR + 1, 2 * B])
        CST = sb("CST", [PART, 2 * B])
        conv_rep = sb("conv_rep", [PART, C, KS * KS])
        conv_out = sb("conv_out", [PART, C * KS * KS])
        member = sb("member", [PART, NPAIR, 2, ROWS])
        group = sb("group", [PART, NPAIR])
        of_group = sb("of_group", [PART, NPAIR, 2])
        conv_bias = sb("conv_bias", [PART, 1])
        conv_mean = sb("conv_mean", [PART, 1])
        conv_abs = sb("conv_abs", [PART, C * KS * KS])
        conv_sum = sb("conv_sum", [PART, 1])
        conv_neg = sb("conv_neg", [PART, C, KS * KS])
        conv_sign = sb("conv_sign", [PART, C, KS * KS])
        diag = sb("diag", [PART, KS, C, ROWS])
        mask = sb("mask", [PART, KS, ROWS])
        band_tap = sb("band_tap", [PART, KS, ROWS, C])
        band_sum = sb("band_sum", [PART, ROWS, C])
        BAND = sb("BAND", [PART, KS, ROWS, C], F32R)

        CN = sb("CN", [PART, 2, 2, NP])

        with ExitStack() as use:
            NAT = sb("NAT", [PART, NPAIR, B, 2, NC, D], F32, use)
        with ExitStack() as use:
            XFIN = sb("XFIN", [PART, 2, DC, B, N], F32, use)
            OUTT = sb("OUTT", [PART, B, NC, D], F32, use)
        XC = sb("XC", [PART, B, NBLK, NP])

        HR = sb("HR", [PART, 2, TOK])
        with ExitStack() as use:
            Ch = sb("Ch", [PART, CRING, 2, NP], F32R, use)
            Cl = sb("Cl", [PART, CRING, 2, NP], F32R, use)
        Hh = sb("Hh", [PART, RING, TOK], F32R)
        Hl = sb("Hl", [PART, RING, TOK], F32R)

        G1 = [bank(f"G1_{i}") for i in range(2)]
        ACC = [[bank(f"ACC_{i}_{m}") for m in range(DC)] for i in range(2)]
        STAT = bank("STAT")
        TR = bank("TR")
        ROT = [ACC[1][0], ACC[1][1], ACC[0][0], ACC[0][1]]

        x_first = [sem(f"x_first{i}") for i in range(2 * B)]
        x_in = [sem(f"x_in{g}") for g in range(1, NPAIR)]
        w1_in, w2_in, bias_in, conv_in = sem("w1_in"), sem("w2_in"), sem("bias_in"), sem("conv_in")
        consts, diag_zero = sem("consts"), sem("diag_zero")
        in_tr, in_evac_act, in_evac_dve = sem("in_tr"), sem("in_evac_act"), sem("in_evac_dve")
        bias_tr, bias_t = sem("bias_tr"), sem("bias_t")
        bn_done, mv_done, mean_mm, dm_done = sem("bn_done"), sem("mv_done"), sem("mean_mm"), sem("dm_done")
        q_done, var_mm, ve_done, rs_done, st_done = (sem("q_done"), sem("var_mm"), sem("ve_done"), sem("rs_done"),
                                                     sem("st_done"))
        whi, wlo = sem("whi"), sem("wlo")
        xn_done, xhi, xlo = sem("xn_done"), sem("xhi"), sem("xlo")
        g1_done, gelu_done, hhi, hlo, g2_done = (sem("g1_done"), sem("gelu_done"), sem("hhi"), sem("hlo"),
                                                 sem("g2_done"))
        evicted = sem("evicted")
        prep = sem("prep")
        x1_out, xc_in = sem("x1_out"), sem("xc_in")
        x1_last = [sem(f"x1_last{b}") for b in range(B)]
        xc_last = [sem(f"xc_last{b}") for b in range(B)]
        cst_done, pads = sem("cst_done"), sem("pads")
        cn_done, chi, clo, conv_mm, cscaled, cadded = (sem("cn_done"), sem("chi"), sem("clo"), sem("conv_mm"),
                                                       sem("cscaled"), sem("cadded"))
        x2_out = [[sem(f"x2_out{b}_{n}") for n in range(len(STORED))] for b in range(B)]
        x2_in = [sem(f"x2_in{b}") for b in range(B)]
        out_tr, out_evac = sem("out_tr"), sem("out_evac")
        out_st = [sem(f"out_st{b}") for b in range(B)]

        block = ctx.enter_context(nc.Block())

        def wait(eng, s, value):
            if not isinstance(value, int) or value > 0:
                eng.wait_ge(s, value)

        def acc(E, ee, b):
            return ACC[(ee + b) % 2 if known(E) == C - 1 else ee]

        def batch_of(E, t):
            return t // HT if units(E) > HT else None

        def width(b):
            return TOK if b is None else N

        def bank_of(i):
            return ROT[i] if i < 4 else ROT[i % 2] if i < 8 else TR

        def evacuated(i):
            return (in_evac_dve, i // 2 - 2) if i % 2 == 0 else (in_evac_act, i // 2 + 3)

        @block.sync
        def _(sp):
            def load_x(g):
                for b in range(B):
                    sp.dma_start(NAT[:, g, b], x[b, 2 * g:2 * g + 2].rearrange("e (c p) d -> p e c d", p=PART)
                                 ).then_inc(x_in[g - 1], 16)

            def load_w1(f, e, E):
                wait(sp, wlo, 8 * E - 4)
                sp.dma_start(W1raw[:], w1[f][e].rearrange("(c p) h -> p c h", p=PART)).then_inc(w1_in, 16)

            def load_w2(f, e, E):
                wait(sp, wlo, 8 * E)
                sp.dma_start(W2raw[:], w2[f][e].rearrange("(t p) d -> p t d", p=PART)).then_inc(w2_in, 16)

            for i in range(2 * B):
                e, b = divmod(i, B)
                sp.dma_start(NAT[:, 0, b, e], x[b, e].rearrange("(c p) d -> p c d", p=PART)).then_inc(x_first[i], 16)
            load_w1(0, 0, 0)
            for f in range(LAYERS):
                sp.dma_start(bias_rows[0:C * HT, f, :], b1[f].rearrange("e (t p) -> (e t) p", p=PART)
                             ).then_inc(bias_in, 16)
                sp.dma_start(bias_rows[C * HT:BCOLS, f, :], b2[f].rearrange("e (c p) -> (e c) p", p=PART)
                             ).then_inc(bias_in, 16)
            load_w2(0, 0, 0)
            load_x(1)
            load_w1(0, 1, 1)
            for i in range(C):
                sp.dma_start(conv_rep[i:PART:C], cw[:, i].rearrange("o a b -> o (a b)").unsqueeze(0)
                             .broadcast_to([ROWS, C, KS * KS])).then_inc(conv_in, 16)
            sp.dma_start(conv_out[:], cw.rearrange("o i a b -> o (i a b)").unsqueeze(0)
                         .broadcast_to([ROWS, C, C * KS * KS])).then_inc(conv_in, 16)
            sp.dma_start(conv_bias[:], cb.unsqueeze(0).unsqueeze(2).broadcast_to([ROWS, C, 1])
                         ).then_inc(conv_in, 16)
            load_x(2)
            load_w2(0, 1, 1)
            load_x(3)

            def store_x1(e, bs, done):
                sp.wait_ge(evicted, evicts(e + 1) - (DC if bs == (0,) else 0))
                cols = slice(bs[0] * N, (bs[-1] + 1) * N)
                rows = x1_dram[e, :, cols].rearrange("r (b n) -> r b n", n=N)
                for i, b in enumerate(bs):
                    sp.dma_start(rows[1:D + 1, i].rearrange("(c p) n -> p c n", p=PART), XT[:, :, b, e]
                                 ).then_inc(done, 16)
                sp.dma_start(rows[0:1], XT[0:1, 0, bs[0]:bs[-1] + 1, e]).then_inc(done, 16)
                sp.dma_start(rows[D + 1:DP], XT[PART - 1:PART, DC - 1, bs[0]:bs[-1] + 1, e]).then_inc(done, 16)

            def load_xc(e, bs, stored, value, done):
                if e == 0:
                    sp.wait_ge(in_tr, B * C)
                sp.wait_ge(stored, value)
                all_rows = slice(e, PART, C)
                written, further = slice(e, OUTR * C, C), slice(OUTR * C + e, PART, C)
                last = NBLK - 1
                for b in bs:
                    rows = x1_dram[e, :, b * N:(b + 1) * N]
                    sp.dma_start(XC[written, b, 0:last, 1:N + 1],
                                 rows[0:OUTR * last].rearrange("(k j) n -> j k n", j=OUTR)).then_inc(done, 16)
                    sp.dma_start(XC[further, b, 0:last - 1, 1:N + 1],
                                 rows[OUTR:OUTR * last].rearrange("(k j) n -> j k n", j=OUTR)[0:KS - 1]
                                 ).then_inc(done, 16)
                    sp.dma_start(XC[further, b, last - 1, 1:N + 1], rows[OUTR * last:OUTR * last + KS - 1]
                                 ).then_inc(done, 16)
                    sp.dma_start(XC[all_rows, b, last, 1:N + 1], rows[LASTROW:DP]).then_inc(done, 16)

            for E in range(2, C + 1):
                f, e = divmod(E, C)
                if E >= 3:
                    store_x1(E - 3, (0, 1), x1_out)
                load_w1(f, e, E)
                if E >= 3:
                    load_xc(E - 3, (0, 1), x1_out, 64 * (E - 2), xc_in)
                load_w2(f, e, E)
            store_x1(C - 2, (0, 1), x1_out)
            load_xc(C - 2, (0, 1), x1_out, 64 * (C - 1), xc_in)
            for b in range(B):
                store_x1(C - 1, (b,), x1_last[b])
                load_xc(C - 1, (b,), x1_last[b], 48, xc_last[b])
                if b == 0:
                    load_w1(1, 1, C + 1)
                    load_w2(1, 1, C + 1)

            def read_x2(b, n):
                sp.wait_ge(x2_out[b][n], 16 * (-(-STORED[n] // 2) - (STORED[n - 1] // 2 if n else 0)))
                for k, blocks, j, nj, c, p0 in pieces_back():
                    if k < STORED[n] and (n == 0 or k >= STORED[n - 1]):
                        sp.dma_start(XT[p0:p0 + blocks * nj, c, b],
                                     x2_dram[b, k:k + blocks, j:j + nj].rearrange("k j o n -> k j (o n)")
                                     ).then_inc(x2_in[b], 16)

            for b in range(B):
                for i in range(TILES):
                    sp.wait_ge(cadded, b * TILES + i + 1)
                    own = slice(2 * i, min(2 * i + 2, NBLK))
                    n = sum(2 * i >= end for end in STORED)
                    sp.dma_start(x2_dram[b, own].rearrange("k j o n -> (j o) k n"), XC[:, b, own, 1:N + 1]
                                 ).then_inc(x2_out[b][n], 16)
                    for n, (end, tile) in enumerate(GROUPS):
                        if i == tile:
                            read_x2(b, n)

            with sp.Fori(2, C) as e:
                load_w1(1, e, C + e)
                load_w2(1, e, C + e)

            def store_out(e, b, n):
                wait(sp, out_evac, 2 * n - 1 + b)
                sp.dma_start(out[b, e].rearrange("(c p) d -> p c d", p=PART), OUTT[:, b]).then_inc(out_st[b], 16)

            with sp.Fori(0, 3) as e:
                load_w1(2, e, 2 * C + e)
                load_w2(2, e, 2 * C + e)
            with sp.Fori(3, C) as e:
                load_w1(2, e, 2 * C + e)
                store_out(e - 3, 0, e - 2)
                load_w2(2, e, 2 * C + e)
                store_out(e - 3, 1, e - 2)
            for e in range(C - 3, C):
                for b in range(B):
                    store_out(e, b, e + 1)
            for b in range(B):
                sp.wait_ge(out_st[b], 16 * C)

        @block.gpsimd
        def _(pool):
            nc.gpsimd.memset(ident[:], 0.0).then_inc(diag_zero, 1)
            nc.gpsimd.memset(ones_mean[:], 1.0 / PART).then_inc(consts, 1)
            nc.gpsimd.memset(half[:], -0.5).then_inc(consts, 1)
            nc.gpsimd.memset(diag[:], 0.0).then_inc(diag_zero, 1)
            nc.gpsimd.memset(member[:], 0.0).then_inc(diag_zero, 1)
            pool.wait_ge(diag_zero, 1)
            nc.gpsimd.affine_select(out=ident[:], in_=ident[:], compare_op=ALU.not_equal, fill=1.0, base=0,
                                    pattern=[[-1, PART]], channel_multiplier=1).then_inc(consts, 1)
            pool.wait_ge(diag_zero, 3)
            for kw in range(KS):
                nc.gpsimd.affine_select(out=diag[:, kw], in_=diag[:, kw], compare_op=ALU.not_equal, fill=1.0,
                                        base=C * (1 - kw), pattern=[[-1, C], [-C, ROWS]], channel_multiplier=1
                                        ).then_inc(consts, 1)
            nc.gpsimd.affine_select(out=member[:], in_=member[:], compare_op=ALU.not_equal, fill=1.0, base=0,
                                    pattern=[[-2, NPAIR], [-1, 2], [-C, ROWS]], channel_multiplier=1
                                    ).then_inc(consts, 1)

            def rstd(J, bs=slice(0, B)):
                wait(pool, ve_done, J + 1)
                nc.gpsimd.tensor_tensor(RS[:, bs], VE[:, bs], half[:, bs], ALU.pow).then_inc(rs_done, 1)

            def normalise_tile(q):
                b, i = divmod(q, TILES)
                own = slice(2 * i, min(2 * i + 2, NBLK))
                wait(pool, clo, q - 1)
                nc.gpsimd.tensor_scalar(CN[:, q % 2, 0:own.stop - own.start], XC[:, b, own], CST[:, b:b + 1],
                                        CST[:, B + b:B + b + 1], ALU.mult, ALU.add).then_inc(cn_done, 1)

            with pool.Fori(0, 7) as J:
                rstd(J)
            rstd(7, slice(0, 1))
            for q in range(B * TILES):
                if q % TILES == 0:
                    pool.wait_ge(cst_done, 2 + 2 * (q // TILES))
                    pool.wait_ge(pads, 2 + 2 * (q // TILES))
                normalise_tile(q)
                if q == 7:
                    rstd(8, slice(1, 2))
                if q == 19:
                    rstd(9, slice(0, 1))
            rstd(10, slice(1, 2))
            with pool.Fori(11, 3 + 4 * NPAIR - 1) as J:
                rstd(J)

        @block.scalar
        def _(act):
            def x_evac(i):
                e, b = divmod(i, B)
                act.wait_ge(in_tr, i + 1)
                if i < 4:
                    act.wait_ge(bn_done, i + 1)
                src = bank_of(i)
                nc.scalar.activation(XT[:, :, b, e], src[:].rearrange("p (c n) -> p c n", c=DC), ACT.Copy
                                     ).then_inc(in_evac_act, 1)

            def w_hi(E, par, k, layer):
                if k < 4:
                    wait(act, w1_in, 16 * (E + 1))
                    wait(act, g1_done, slots(E - 1, layer) if known(E) != C + 2 else slots(E) - HT)
                    c, hh = divmod(k, 2)
                    at = slice(hh * 512, hh * 512 + 512)
                    dst, src = W1h[:, par, c, at], W1raw[:, c, at]
                else:
                    wait(act, w2_in, 16 * (E + 1))
                    wait(act, g2_done, slots(E - 1, layer) if known(E) != C + 2 else slots(E) - HT)
                    at = slice(2 * (k - 4), 2 * (k - 4) + 2)
                    dst, src = W2h[:, par, at], W2raw[:, at]
                nc.scalar.activation(dst, src, ACT.Copy).then_inc(whi, 1)

            def x_hi(E, par, b, layer):
                wait(act, xn_done, norm_of(E, b) + 1)
                wait(act, g1_done, slots(E - 1, layer) if known(E) != C + 2 else slot_of(C, (b + 1) * HT - 1) + 1)
                nc.scalar.activation(Xh[:, par, :, b], XN[:, b], ACT.Copy).then_inc(xhi, 1)

            def gelu(E, t, func, col, layer):
                s, n = slot_of(E, t, layer), width(batch_of(E, t))
                wait(act, g1_done, s + 1)
                wait(act, hlo, s - 1)
                nc.scalar.activation(HR[:, t % 2, 0:n], G1[t % 2][:, 0:n], func, bias=BT[:, bass.ds(col, 1)]
                                     ).then_inc(gelu_done, 1)
                wait(act, gelu_done, s + 1)
                wait(act, g2_done, s - RING + 1)
                nc.scalar.activation(Hh[:, t % RING, 0:n], HR[:, t % 2, 0:n], ACT.Copy).then_inc(hhi, 1)

            def out_evac_step(E, b, src=TR):
                n = E - 2 * C
                wait(act, out_tr, 2 * n + b + 1)
                wait(act, out_st[b], 16 * n)
                nc.scalar.activation(OUTT[:, b].rearrange("p c d -> p (c d)"), src[:], ACT.Copy
                                     ).then_inc(out_evac, 1)

            def pair(P, f, func):
                for ee, t in order(P):
                    E, e = 2 * P + ee, 2 * (P - NPAIR * f) + ee
                    norms = norms_of(P, ee, f)
                    gelu(E, t, func, BCOLS * f + HT * e + t % HT, f)
                    if known(E) == 0 and t in (0, 2):
                        x_evac(4 + t)
                    k = split_at(P, ee, t)
                    if k is not None:
                        w_hi(E + 1, 1 - ee, k, f)
                    if t in norms:
                        En, b, J = norms[t]
                        x_hi(En, En % 2 if isinstance(En, int) else 1 - ee, b, f)
                    if known(E) == 1 and t % 2 == 0:
                        x_evac(8 + t)
                    if f == 2 and t in (5, 7):
                        if not isinstance(P, int) or E > 2 * C:
                            out_evac_step(E - 1, (t - 5) // 2)

            act.wait_ge(consts, 2)
            nc.scalar.activation(gelu_table[:], half[:], ACT.Gelu_apprx_tanh)
            for i in range(4):
                x_evac(i)
            for k in range(4):
                w_hi(0, 0, k, 0)
            for b in range(B):
                x_hi(0, 0, b, 0)
            for k in range(4, 8):
                w_hi(0, 0, k, 0)
            act.wait_ge(bias_t, 1)
            pair(0, 0, ACT.Gelu_apprx_tanh)
            with act.Fori(1, 3) as P:
                pair(P, 0, ACT.Gelu_apprx_tanh)
            pair(3, 0, ACT.Gelu_apprx_tanh)

            act.wait_ge(prep, 5 + KS)
            act.wait_ge(g2_done, slots(C))
            for q in range(B * TILES + 2):
                if q < B * TILES:
                    w = 1 if q % TILES == TILES - 1 else 2
                    wait(act, cn_done, q + 1)
                    wait(act, conv_mm, q - CRING + 1)
                    nc.scalar.activation(Ch[:, q % CRING, 0:w], CN[:, q % 2, 0:w], ACT.Copy).then_inc(chi, 1)
                if q >= 2:
                    w = N if (q - 2) % TILES == TILES - 1 else 2 * N
                    wait(act, conv_mm, q - 1)
                    bank_q = ROT[(q - 2) % 4][:, 0:w]
                    nc.scalar.activation(bank_q, bank_q, ACT.Identity, bias=conv_bias[:, 0:1],
                                         scale=conv_mean[:, 0:1]).then_inc(cscaled, 1)
            x_hi(C, 0, 0, 1)
            for k in range(4):
                w_hi(C + 1, 1, k, 1)

            pair(4, 1, ACT.Gelu_apprx_tanh)
            with act.Fori(5, 7) as P:
                pair(P, 1, ACT.Gelu_apprx_tanh)
            pair(7, 1, ACT.Gelu_apprx_tanh)
            pair(8, 2, ACT.Gelu)
            with act.Fori(9, 11) as P:
                pair(P, 2, ACT.Gelu)
            pair(11, 2, ACT.Gelu)
            for b in range(B):
                out_evac_step(3 * C - 1, b, (TR, G1[0])[b])

        @block.vector
        def _(dve):
            def x_evac(i):
                e, b = divmod(i, B)
                dve.wait_ge(in_tr, i + 1)
                nc.vector.tensor_copy(XT[:, :, b, e], bank_of(i)[:].rearrange("p (c n) -> p c n", c=DC)
                                      ).then_inc(in_evac_dve, 1)

            def sums(J, e, bs=None):
                for b in bs or batches(J):
                    for i in range(2):
                        at = XT[:, :, b, e + i] if isinstance(e, int) else XT[:, :, b, bass.ds(e + i, 1)]
                        nc.vector.bn_stats(BN[:, b, i], at).then_inc(bn_done, 1)

            def sums_done(J, late=False):
                wait(dve, bn_done, 2 * (jobs_weighed(J, late) + len(batches(J))))

            def aggregate(J):
                for b in batches(J):
                    nc.vector.bn_aggr(MV[:, b], BN[:, b].rearrange("p i s -> p (i s)")).then_inc(mv_done, 1)

            def deviate(J):
                bs = batches(J)
                own = slice(bs[0], bs[-1] + 1)
                wait(dve, mean_mm, J + 1)
                nc.vector.tensor_copy(MEAN[:, own], STAT[:, own])
                nc.vector.tensor_tensor(DM[:, own], MV[:, own, 0], STAT[:, own], ALU.subtract).then_inc(dm_done, 1)
                wait(dve, dm_done, J + 1)
                for b in bs:
                    nc.vector.scalar_tensor_tensor(Q[:, b:b + 1], DM[:, b:b + 1], DM[:, b:b + 1], MV[:, b, 1:2],
                                                   ALU.mult, ALU.add).then_inc(q_done, 1)

            def add_eps(J):
                bs = batches(J)
                wait(dve, var_mm, J + 1)
                nc.vector.tensor_scalar(VE[:, bs[0]:bs[-1] + 1], STAT[:, B + bs[0]:B + bs[-1] + 1], GN_EPS, None,
                                        ALU.add).then_inc(ve_done, 1)

            def scale_shift(J, slot):
                bs = batches(J)
                own = slice(bs[0], bs[-1] + 1)
                wait(dve, rs_done, J + 1)
                at = slice(slot, slot + 1) if isinstance(slot, int) else bass.ds(slot, 1)
                nc.vector.tensor_copy(ST[:, at, own], RS[:, own].unsqueeze(1))
                nc.vector.scalar_tensor_tensor(ST[:, at, B + bs[0]:B + bs[-1] + 1], MEAN[:, own].unsqueeze(1), -1.0,
                                               RS[:, own].unsqueeze(1), ALU.mult, ALU.mult).then_inc(st_done, 1)

            def w_lo(E, par, k):
                wait(dve, whi, 8 * E + k + 1)
                if k < 4:
                    c, hh = divmod(k, 2)
                    at = slice(hh * 512, hh * 512 + 512)
                    dst, src, high = W1l[:, par, c, at], W1raw[:, c, at], W1h[:, par, c, at]
                else:
                    at = slice(2 * (k - 4), 2 * (k - 4) + 2)
                    dst, src, high = W2l[:, par, at], W2raw[:, at], W2h[:, par, at]
                nc.vector.tensor_tensor(dst, src, high.bitcast(F32), ALU.subtract).then_inc(wlo, 1)

            def norm(E, e, b, J):
                m = norm_of(E, b)
                wait(dve, st_done, J + 1)
                before = m if known(E) == C + 1 else m - 1
                wait(dve, xhi, before)
                wait(dve, xlo, before)
                at = XT[:, :, b, e] if isinstance(e, int) else XT[:, :, b, bass.ds(e, 1)]
                nc.vector.tensor_scalar(XN[:, b], at, ST[:, NPAIR, b:b + 1], ST[:, NPAIR, B + b:B + b + 1], ALU.mult,
                                        ALU.add).then_inc(xn_done, 1)

            def x_lo(E, par, b):
                wait(dve, xhi, norm_of(E, b) + 1)
                nc.vector.tensor_tensor(Xl[:, par, :, b], XN[:, b], Xh[:, par, :, b].bitcast(F32), ALU.subtract
                                        ).then_inc(xlo, 1)

            def h_lo(E, t, layer):
                n = width(batch_of(E, t))
                wait(dve, hhi, slot_of(E, t, layer) + 1)
                nc.vector.tensor_tensor(Hl[:, t % RING, 0:n], HR[:, t % 2, 0:n],
                                        Hh[:, t % RING, 0:n].bitcast(F32), ALU.subtract).then_inc(hlo, 1)

            def evict(E, par, e, f, b=None):
                halved = known(E) in HALVED
                wait(dve, g2_done, slot_of(E, (b + 1) * HT - 1 if halved else HT - 1, f) + 1)
                if f == 2:
                    wait(dve, out_tr, 2 * (E - 2 * C) - 2)
                cols = slice(0, width(b)) if halved or b is None else slice(b * N, (b + 1) * N)
                for m in range(DC):
                    bs = slice(0, B) if b is None else slice(b, b + 1)
                    at = XT[:, m, bs, e] if isinstance(e, int) else XT[:, m, bs, bass.ds(e, 1)]
                    dst = XFIN[:, par, m, bs] if f == 2 else at
                    nc.vector.scalar_tensor_tensor(
                        dst, acc(E, par, b or 0)[m][:, cols].rearrange("p (b n) -> p b n", n=N),
                        BT[:, bass.ds(BCOLS * f + C * HT + DC * e + m, 1)],
                        at, ALU.add, ALU.add).then_inc(evicted, 1)

            def to_partitions(b):
                nc.vector.tensor_tensor(of_group[:], ST[:, 0:NPAIR, b:2 * B:B],
                                        group[:].unsqueeze(2).broadcast_to([PART, NPAIR, 2]), ALU.mult
                                        ).then_inc(cst_done, 1)
                dve.wait_ge(cst_done, 2 * b + 1)
                nc.vector.tensor_reduce(CST[:, b:2 * B:B], of_group[:].rearrange("p g s -> p s g"), AX.X, ALU.add
                                        ).then_inc(cst_done, 1)

            def double_edges(b):
                dve.wait_ge(xc_in, 16 * 8 * (C - 1))
                dve.wait_ge(xc_last[b], 16 * 4)
                nc.vector.tensor_copy(XC[:, b, :, 0:1], XC[:, b, :, 1:2]).then_inc(pads, 1)
                nc.vector.tensor_copy(XC[:, b, :, NP - 1:NP], XC[:, b, :, N:N + 1]).then_inc(pads, 1)

            def signs_and_means():
                dve.wait_ge(conv_in, 16 * (C + 2))
                dve.wait_ge(consts, 4 + KS)
                nc.vector.tensor_scalar(conv_neg[:], conv_rep[:], 0.0, None, ALU.is_lt).then_inc(prep, 1)
                nc.vector.scalar_tensor_tensor(conv_abs[:], conv_out[:], -1.0, conv_out[:], ALU.mult, ALU.max,
                                               accum_out=conv_sum[:]).then_inc(prep, 1)
                for kw in range(KS):
                    nc.vector.tensor_reduce(mask[:, kw], diag[:, kw].rearrange("p c j -> p j c"), AX.X, ALU.add
                                            ).then_inc(prep, 1)
                nc.vector.tensor_reduce(group[:], member[:].rearrange("p g i j -> p g (i j)"), AX.X, ALU.add
                                        ).then_inc(prep, 1)
                dve.wait_ge(prep, 3 + KS)
                nc.vector.scalar_tensor_tensor(conv_sign[:], conv_rep[:], 0.0, conv_neg[:], ALU.is_gt, ALU.subtract
                                               ).then_inc(prep, 1)
                nc.vector.tensor_scalar(conv_mean[:], conv_sum[:], 1.0 / (C * KS * KS), None, ALU.mult
                                        ).then_inc(prep, 1)

            def band(kh):
                before = 5 + KS + kh * (KS + 2)
                dve.wait_ge(prep, before)
                sign = conv_sign[:].rearrange("p o (a b) -> p a b o", a=KS)
                for kw in range(KS):
                    nc.vector.tensor_tensor(band_tap[:, kw],
                                            sign[:, kh, kw:kw + 1].broadcast_to([PART, ROWS, C]),
                                            mask[:, kw].unsqueeze(2).broadcast_to([PART, ROWS, C]), ALU.mult
                                            ).then_inc(prep, 1)
                dve.wait_ge(prep, before + KS)
                nc.vector.tensor_tensor(band_sum[:], band_tap[:, 0], band_tap[:, 1], ALU.add).then_inc(prep, 1)
                dve.wait_ge(prep, before + KS + 1)
                nc.vector.tensor_tensor(BAND[:, kh], band_sum[:], band_tap[:, 2], ALU.add).then_inc(prep, 1)

            def pair(P, f):
                for ee, t in order(P):
                    E, e = 2 * P + ee, 2 * (P - NPAIR * f) + ee
                    jobs, norms = jobs_of(P, ee, f), norms_of(P, ee, f)
                    for J, steps, src, slot in jobs:
                        if steps.get("aggregate") == t and steps["sums"] != t:
                            sums_done(J, f > 0)
                    if known(E) in CROSSED and t % HT == 2:
                        if (ee, t) != (0, 2):
                            evict(E - 1 if ee else E + 1, 1 - ee, 1 - ee, f, t // HT if ee else 0)
                    elif known(E) == C + 2 and t == 2:
                        evict(E - 1, 1, e - 1, f, 1)
                    elif t == 2 and known(E) != 0:
                        if known(E) == 2 * C:
                            evict(E - 1, 1 - ee, C - 1, 1)
                        else:
                            evict(E - 1, 1 - ee, e - 1, f)
                    elif t == HT + 2:
                        evict(E, ee, e, f, 0)
                    h_lo(E, t, f)
                    if known(E) == 0 and t in (1, 3):
                        x_evac(4 + t)
                    k = split_at(P, ee, t)
                    if k is not None:
                        w_lo(E + 1, 1 - ee, k)
                    for J, steps, src, slot in jobs:
                        if steps.get("sums") == t:
                            if known(E) == 0:
                                for i in (7, 8):
                                    dve.wait_ge(*evacuated(i))
                            if known(J) == 10:
                                dve.wait_ge(x2_in[1], 16 * len(pieces_back()))
                            if known(J) == 7:
                                dve.wait_ge(evicted, evicts(C) - DC)
                            elif f == 0 and ee:
                                wait(dve, evicted, evicts(2 * P, 0))
                            elif known(P) == 7 or f == 2:
                                wait(dve, evicted, evicts(2 * P - 4, 1))
                            sums(J, src, (0,) if "more_sums" in steps else None)
                        if steps.get("more_sums") == t:
                            sums(J, src, (1,))
                        if steps.get("aggregate") == t:
                            if steps["sums"] == t:
                                sums_done(J, f > 0)
                            aggregate(J)
                        if steps.get("deviate") == t:
                            deviate(J)
                        if steps.get("eps") == t:
                            add_eps(J)
                        if steps.get("scale") == t:
                            scale_shift(J, slot)
                    if t + 1 in norms:
                        En, b, J = norms[t + 1]
                        norm(En, En % C if isinstance(En, int) else e + 1, b, J)
                    if t in norms:
                        En, b, J = norms[t]
                        x_lo(En, En % 2 if isinstance(En, int) else 1 - ee, b)
                    if known(E) == 1 and t % 2 == 1:
                        x_evac(8 + t)
                    if known(E) == 1 and t == 6:
                        signs_and_means()
                    if known(E) == C - 2 and t in (2, 6):
                        band(1 if t == 2 else 2)
                    if known(E) == C - 1 and t == 14:
                        dve.wait_ge(st_done, 8)
                        to_partitions(0)

            for i in range(4):
                e, b = divmod(i, B)
                dve.wait_ge(in_tr, i + 1)
                nc.vector.bn_stats(BN[:, b, e], ROT[i][:]).then_inc(bn_done, 1)
            sums_done(0)
            aggregate(0)
            deviate(0)
            w_lo(0, 0, 0)
            add_eps(0)
            w_lo(0, 0, 1)
            scale_shift(0, NPAIR)
            dve.wait_ge(in_evac_act, B * 2)
            for b in range(B):
                norm(0, 0, b, 0)
            for b in range(B):
                w_lo(0, 0, 2 + b)
                x_lo(0, 0, b)
            dve.wait_ge(bias_tr, LAYERS)
            nc.vector.tensor_copy(BT[:], TR[:, 0:LAYERS * BCOLS]).then_inc(bias_t, 1)
            for k in range(4, 8):
                w_lo(0, 0, k)
            dve.wait_ge(bias_t, 1)
            pair(0, 0)

            band(0)
            for i in (B * C - 1, B * C):
                dve.wait_ge(*evacuated(i))
            with dve.Fori(1, 3) as P:
                pair(P, 0)
            pair(3, 0)
            double_edges(0)

            def conv_low(q):
                w = 1 if q % TILES == TILES - 1 else 2
                wait(dve, chi, q + 1)
                nc.vector.tensor_tensor(Cl[:, q % CRING, 0:w], CN[:, q % 2, 0:w],
                                        Ch[:, q % CRING, 0:w].bitcast(F32), ALU.subtract).then_inc(clo, 1)

            def conv_add(q):
                b, i = divmod(q, TILES)
                own = slice(2 * i, min(2 * i + 2, NBLK))
                w = own.stop - own.start
                wait(dve, cscaled, q + 1)
                at = XC[:, b, own, 1:N + 1]
                nc.vector.tensor_tensor(at, ROT[q % 4][:, 0:w * N].rearrange("p (k n) -> p k n", k=w),
                                        at, ALU.add).then_inc(cadded, 1)

            for q in range(B * TILES - 3):
                conv_low(q)
                if q >= 2:
                    conv_add(q - 2)
                if q == 1:
                    evict(C - 1, 1, C - 1, 0, 1)
                if q == 2:
                    dve.wait_ge(evicted, evicts(C))
                    sums(8, C - 2)
                if q == 3:
                    sums_done(8)
                    aggregate(8)
                if q == 4:
                    deviate(8)
                if q == 6:
                    add_eps(8)
                if q == 7:
                    scale_shift(8, NPAIR - 1)
                    dve.wait_ge(st_done, 9)
                    to_partitions(1)
                    double_edges(1)
            q = B * TILES
            conv_low(q - 3)
            dve.wait_ge(x2_in[0], 16 * len(pieces_back()))
            sums(9, 0)
            sums_done(9)
            aggregate(9)
            conv_add(q - 5)
            conv_low(q - 2)
            deviate(9)
            conv_add(q - 4)
            add_eps(9)
            conv_low(q - 1)
            scale_shift(9, NPAIR)
            norm(C, 0, 0, 9)
            conv_add(q - 3)
            x_lo(C, 0, 0)
            conv_add(q - 2)
            conv_add(q - 1)
            for k in range(4):
                w_lo(C + 1, 1, k)

            pair(4, 1)
            for P in range(5, 8):
                pair(P, 1)
            pair(8, 2)
            with dve.Fori(9, 11) as P:
                pair(P, 2)
            pair(11, 2)
            for b in range(B):
                evict(3 * C - 1, 1, C - 1, 2, b)

        @block.tensor
        def _(pe):
            def x_transpose(i):
                e, b = divmod(i, B)
                if i < 2 * B:
                    pe.wait_ge(x_first[i], 16)
                elif i % (2 * B) == 0:
                    pe.wait_ge(x_in[e // 2 - 1], 32)
                if i in (6, 7):
                    pe.wait_ge(*evacuated(i - 1))
                if i == 8:
                    pe.wait_ge(bias_t, 1)
                if i > 8:
                    pe.wait_ge(*evacuated(i))
                dst = bank_of(i)
                for c in range(DC):
                    for r in range(NC):
                        at = c * N + r * PART
                        ins = nc.tensor.transpose(dst[:, at:at + PART],
                                                  NAT[:, e // 2, b, e % 2, r, c * PART:(c + 1) * PART], ident[:])
                ins.then_inc(in_tr, 1)

            def stay_busy(n):
                for _ in range(n):
                    nc.tensor.matmul(G1[1][:, 0:PART], ident[:], ones_mean[:], start=True, stop=True)

            def mean_over_partitions(J, late=False):
                bs = batches(J)
                wait(pe, mv_done, jobs_weighed(J, late) + len(bs))
                wait(pe, ve_done, J)
                nc.tensor.matmul(STAT[:, bs[0]:bs[-1] + 1], ones_mean[:], MV[:, bs[0]:bs[-1] + 1, 0], start=True,
                                 stop=True).then_inc(mean_mm, 1)

            def variance_over_partitions(J, late=False):
                bs = batches(J)
                wait(pe, q_done, jobs_weighed(J, late) + len(bs))
                nc.tensor.matmul(STAT[:, B + bs[0]:B + bs[-1] + 1], ones_mean[:], Q[:, bs[0]:bs[-1] + 1], start=True,
                                 stop=True).then_inc(var_mm, 1)

            def g1(E, ee, t, layer):
                b = batch_of(E, t)
                wait(pe, gelu_done, slot_of(E, t, layer) - 1)
                if t % HT == 0:
                    wait(pe, xlo, norm_of(E, B - 1 if b is None else b) + 1)
                    wait(pe, wlo, 8 * E + 4)
                t8 = t % HT
                col = slice(t8 * PART, (t8 + 1) * PART)
                parts = [(w, xx, c) for c in range(DC) for w, xx in ((W1l, Xh), (W1h, Xl), (W1h, Xh))]
                for n, (w, xx, c) in enumerate(parts):
                    rhs = xx[:, ee, c].rearrange("p b n -> p (b n)") if b is None else xx[:, ee, c, b]
                    ins = nc.tensor.matmul(G1[t % 2][:, 0:width(b)], w[:, ee, c, col], rhs,
                                           start=n == 0, stop=n == len(parts) - 1)
                ins.then_inc(g1_done, 1)

            def g2(E, ee, t, layer):
                b = batch_of(E, t)
                n, s, t8 = width(b), slot_of(E, t, layer), t % HT
                banks = acc(E, ee, b or 0)
                wait(pe, hhi, s + 1)
                if t8 == 0:
                    wait(pe, wlo, 8 * E + 8)
                    wait(pe, evicted, evicts_for(E, b, layer))
                    if known(E) == C:
                        pe.wait_ge(cadded, B * TILES)
                for m in range(DC):
                    col = slice(m * PART, (m + 1) * PART)
                    high = Hh[:, t % RING, 0:n]
                    nc.tensor.matmul(banks[m][:, 0:n], W2l[:, ee, t8, col], high, start=t8 == 0, stop=False)
                    nc.tensor.matmul(banks[m][:, 0:n], W2h[:, ee, t8, col], high, start=False, stop=False)
                wait(pe, hlo, s + 1)
                for m in range(DC):
                    col = slice(m * PART, (m + 1) * PART)
                    ins = nc.tensor.matmul(banks[m][:, 0:n], W2h[:, ee, t8, col], Hl[:, t % RING, 0:n],
                                           start=False, stop=t8 == HT - 1)
                ins.then_inc(g2_done, 1)

            def out_transpose(E, par, b, dst=TR):
                n = E - 2 * C
                wait(pe, evicted, evicts(E + 1, 2) + (b * DC if known(E) == LAYERS * C - 1 else 0))
                if dst is TR:
                    wait(pe, out_evac, 2 * n + b)
                for r in range(NC):
                    for c in range(DC):
                        at = r * D + c * PART
                        ins = nc.tensor.transpose(dst[:, at:at + PART], XFIN[:, par, c, b, r * PART:(r + 1) * PART],
                                                  ident[:])
                ins.then_inc(out_tr, 1)

            def pair(P, f):
                steps_of_pair = order(P)
                for u, (ee, t) in enumerate(steps_of_pair):
                    E = 2 * P + ee
                    g1(E, ee, t, f)
                    if u >= 2:
                        ee2, t2 = steps_of_pair[u - 2]
                        g2(2 * P + ee2, ee2, t2, f)
                    elif not (known(E) in (0, C)):
                        g2(E - 1, 1, t + units(E - 1) - 2, f)
                    for J, steps, src, slot in jobs_of(P, ee, f):
                        if steps.get("mean") == t:
                            mean_over_partitions(J, f > 0)
                        if steps.get("variance") == t:
                            variance_over_partitions(J, f > 0)
                    if known(E) == 0 and t < 4:
                        x_transpose(4 + t)
                    if known(E) == 1:
                        x_transpose(8 + t)
                    if f == 2 and t in (4, 6) and (not isinstance(P, int) or E > 2 * C):
                        out_transpose(E - 1, 1 - ee, t // 2 - 2)

            def drain(E, f):
                for t in (units(E) - 2, units(E) - 1):
                    g2(E, 1, t, f)

            pe.wait_ge(consts, 3)
            stay_busy(5)
            for i in range(4):
                x_transpose(i)
            stay_busy(5)
            mean_over_partitions(0)
            stay_busy(3)
            variance_over_partitions(0)
            pe.wait_ge(bias_in, 16 * 2 * LAYERS)
            for f in range(LAYERS):
                nc.tensor.transpose(TR[:, f * BCOLS:(f + 1) * BCOLS], bias_rows[:, f, :], ident[0:BCOLS, 0:BCOLS]
                                    ).then_inc(bias_tr, 1)
            stay_busy(16)
            pair(0, 0)
            with pe.Fori(1, 3) as P:
                pair(P, 0)
            pair(3, 0)
            drain(C - 1, 0)

            pe.wait_ge(prep, 5 + KS + KS * (KS + 2))
            for q in range(B * TILES):
                w = 1 if q % TILES == TILES - 1 else 2
                if q == 4:
                    mean_over_partitions(8)
                if q == 6:
                    variance_over_partitions(8)
                if q == B * TILES - 2:
                    mean_over_partitions(9)
                if q == B * TILES - 1:
                    variance_over_partitions(9)
                if q == 2:
                    pe.wait_ge(evicted, evicts(C))
                wait(pe, chi, q + 1)
                wait(pe, cadded, q - 3)
                parts = [(xx, kh) for xx in (Ch, Cl) for kh in range(KS)]
                for n, (xx, kh) in enumerate(parts):
                    if n == KS:
                        wait(pe, clo, q + 1)
                    ins = nc.tensor.matmul(ROT[q % 4][:, 0:w * N].rearrange("p (k n) -> p k n", k=w),
                                           BAND[:, kh].rearrange("p j o -> p (j o)"),
                                           xx[:, q % CRING, 0:w, kh:kh + N], start=n == 0, stop=n == len(parts) - 1)
                ins.then_inc(conv_mm, 1)

            pair(4, 1)
            pair(5, 1)
            with pe.Fori(6, 8) as P:
                pair(P, 1)
            pair(8, 2)
            with pe.Fori(9, 11) as P:
                pair(P, 2)
            pair(11, 2)
            drain(3 * C - 1, 2)
            for b in range(B):
                out_transpose(3 * C - 1, 1, b, (TR, G1[0])[b])


_INS = {"x": (B, C, N, D)}
for _l in ("L0", "L2", "L3"):
    _INS.update({f"{_l}_conv_w1": (C, D, H), f"{_l}_conv_b1": (C, H), f"{_l}_conv_w2": (C, H, D),
                 f"{_l}_conv_b2": (C, D)})
_INS.update({"L1_conv_weight": (C, C, KS, KS), "L1_conv_bias": (C,)})


def kernel(**inputs):
    import numpy as np
    import concourse.bacc as bacc
    from concourse.bass_utils import run_bass_kernel_spmd

    nc = bacc.Bacc("TRN2", target_bir_lowering=False, num_devices=1)
    arrays, t = {}, {}
    for name, shape in _INS.items():
        arrays[f"in_{name}"] = np.ascontiguousarray(inputs[name])
        t[name] = nc.dram_tensor(f"in_{name}", shape, F32, kind="ExternalInput").ap()
    out = nc.dram_tensor("out_x", (B, C, N, D), F32, kind="ExternalOutput").ap()
    layers = ("L0", "L2", "L3")
    build(nc, t["x"], *([t[f"{name}_conv_{p}"] for name in layers] for p in ("w1", "b1", "w2", "b2")),
          t["L1_conv_weight"], t["L1_conv_bias"], out)
    r = run_bass_kernel_spmd(nc, [arrays], core_ids=[0])
    return r.results[0]["out_x"]
```
